# Optimizing a Trainium2 kernel written in Bass

```python
import numpy as np
import jax
import jax.numpy as jnp

def _softmax(x, axis=-1):
    return jax.nn.softmax(x, axis=axis)

def _gelu(x):
    return jax.nn.gelu(x, approximate=True)

def _silu(x):
    return jax.nn.silu(x)

def _sigmoid(x):
    return jax.nn.sigmoid(x)

def _layernorm(x, axis=-1, eps=1e-05):
    m = jnp.mean(x, axis=axis, keepdims=True)
    v = jnp.var(x, axis=axis, keepdims=True)
    return (x - m) / jnp.sqrt(v + eps)

def _scatter_add(tgt, idx, src, axis=0):
    return tgt.at[idx].add(src)

def _segment_sum(src, seg, n):
    return jax.ops.segment_sum(src, seg, n)
kernel_name = 'mk_cond_resid_d4_seqx_r4_c06ce8'

def setup_inputs(seed: int=0):
    np.random.seed(seed)
    _w = jnp.asarray

    def _rec_inputs():
        import jax
        import jax.numpy as jnp
        _rk = jax.random.key(seed)
        x = 4.136e-05 + 0.9999 * jax.random.normal(jax.random.fold_in(_rk, 1), (32, 256, 256), jnp.float32)
        _lenS = 256 - jax.random.randint(jax.random.fold_in(_rk, 7), (32,), 0, max(1, 256 // 4) + 1, jnp.int32)
        _lenS2 = 256 - jax.random.randint(jax.random.fold_in(_rk, 8), (32,), 0, max(1, 256 // 4) + 1, jnp.int32)
        cond_1024 = -0.00608245 + 1.00131 * jax.random.normal(jax.random.fold_in(_rk, 11), (32, 256), jnp.float32)
        return (x, cond_1024)
    x, cond_1024 = _rec_inputs()

    def _L0_cond_setup():
        import jax, jax.numpy as jnp
        import numpy as np
        B, T, D_IN, V_IN, E = (64, 128, 256, 256, 256)
        key = jax.random.key(seed)
        ks = jax.random.split(key, 16)
        s = 0.01
        return {'video': jax.random.normal(ks[0], (B, V_IN), jnp.float32), 'seq': jax.random.normal(ks[1], (B, T, D_IN), jnp.float32), 'W_z': jax.random.normal(ks[2], (D_IN, E), jnp.float32) * s, 'U_z': jax.random.normal(ks[3], (E, E), jnp.float32) * s, 'C_z': jax.random.normal(ks[4], (V_IN, E), jnp.float32) * s, 'b_z': jnp.zeros((E,), jnp.float32), 'W_r': jax.random.normal(ks[5], (D_IN, E), jnp.float32) * s, 'U_r': jax.random.normal(ks[6], (E, E), jnp.float32) * s, 'C_r': jax.random.normal(ks[7], (V_IN, E), jnp.float32) * s, 'b_r': jnp.zeros((E,), jnp.float32), 'W': jax.random.normal(ks[8], (D_IN, E), jnp.float32) * s, 'U': jax.random.normal(ks[9], (E, E), jnp.float32) * s, 'C': jax.random.normal(ks[10], (V_IN, E), jnp.float32) * s, 'b': jnp.zeros((E,), jnp.float32)}
    _L0_cond_all = _L0_cond_setup()
    _L0_cond_in = {k: v for k, v in _L0_cond_all.items() if k in ('W_z', 'U_z', 'C_z', 'b_z', 'W_r', 'U_r', 'C_r', 'b_r', 'W', 'U', 'C', 'b')}
    del _L0_cond_all

    def _L1_cond_setup():
        import jax, jax.numpy as jnp
        import numpy as np
        LATENT = 256
        key = jax.random.key(seed)
        k1, k2, k3, k4 = jax.random.split(key, 4)
        B, T, D = (64, 128, LATENT)
        h_t = jax.random.normal(k1, (B, D), dtype=jnp.float32)
        z = jax.random.normal(k2, (B, T, D), dtype=jnp.float32)
        bound = 1.0 / np.sqrt(2 * D)
        W = jax.random.uniform(k3, (D, 2 * D), minval=-bound, maxval=bound, dtype=jnp.float32)
        b = jax.random.uniform(k4, (D,), minval=-bound, maxval=bound, dtype=jnp.float32)
        alpha = jnp.full((D,), 0.1, dtype=jnp.float32)
        return {'h_t': h_t, 'z': z, 'W': W, 'b': b, 'alpha': alpha}
    _L1_cond_all = _L1_cond_setup()
    _L1_cond_in = {k: v for k, v in _L1_cond_all.items() if k in ('W', 'b', 'alpha')}
    del _L1_cond_all

    def _L2_cond_setup():
        import jax, jax.numpy as jnp
        import numpy as np
        EPS = 1e-08
        key = jax.random.key(seed)
        ks = jax.random.split(key, 8)
        B, S, D, H = (8, 512, 256, 256)
        scale = 1.0 / np.sqrt(D)
        return {'input_seq': jax.random.normal(ks[0], (B, S, D), dtype=jnp.float32), 'initial_hidden': jax.random.normal(ks[1], (B, H), dtype=jnp.float32), 'W_f': jax.random.normal(ks[2], (H, D), dtype=jnp.float32) * scale, 'b_f': jnp.zeros((H,), dtype=jnp.float32), 'W_i': jax.random.normal(ks[3], (H, D), dtype=jnp.float32) * scale, 'b_i': jnp.zeros((H,), dtype=jnp.float32), 'W_h': jax.random.normal(ks[4], (H, D), dtype=jnp.float32) * scale, 'b_h': jnp.zeros((H,), dtype=jnp.float32)}
    _L2_cond_all = _L2_cond_setup()
    _L2_cond_in = {k: v for k, v in _L2_cond_all.items() if k in ('W_f', 'b_f', 'W_i', 'b_i', 'W_h', 'b_h')}
    del _L2_cond_all

    def _L3_cond_setup():
        import jax, jax.numpy as jnp
        import numpy as np
        RANK = 8
        LN_EPS = 1e-05
        key = jax.random.key(seed)
        ks = jax.random.split(key, 8)
        B, T, D = (16, 256, 256)
        A = 256
        I = 256
        OUT = D * RANK * 4
        s = 0.02
        return {'x': jax.random.normal(ks[0], (B, T, D), jnp.float32), 'ada_emb': jax.random.normal(ks[1], (B, A), jnp.float32), 'base_up': jax.random.normal(ks[2], (D, D), jnp.float32) * s, 'base_down': jax.random.normal(ks[3], (D, D), jnp.float32) * s, 'ln_gamma': jnp.ones((A,), jnp.float32), 'ln_beta': jnp.zeros((A,), jnp.float32), 'W1': jax.random.normal(ks[4], (A, I), jnp.float32) / np.sqrt(A), 'bias1': jnp.zeros((I,), jnp.float32), 'W2': jax.random.normal(ks[5], (I, OUT), jnp.float32) / np.sqrt(I), 'bias2': jnp.zeros((OUT,), jnp.float32)}
    _L3_cond_all = _L3_cond_setup()
    _L3_cond_in = {k: v for k, v in _L3_cond_all.items() if k in ('base_up', 'base_down', 'ln_gamma', 'ln_beta', 'W1', 'bias1', 'W2', 'bias2')}
    del _L3_cond_all
    return {'x': x, 'cond_1024': cond_1024, 'L0_cond_W_z': _L0_cond_in['W_z'], 'L0_cond_U_z': _L0_cond_in['U_z'], 'L0_cond_C_z': _L0_cond_in['C_z'], 'L0_cond_b_z': _L0_cond_in['b_z'], 'L0_cond_W_r': _L0_cond_in['W_r'], 'L0_cond_U_r': _L0_cond_in['U_r'], 'L0_cond_C_r': _L0_cond_in['C_r'], 'L0_cond_b_r': _L0_cond_in['b_r'], 'L0_cond_W': _L0_cond_in['W'], 'L0_cond_U': _L0_cond_in['U'], 'L0_cond_C': _L0_cond_in['C'], 'L0_cond_b': _L0_cond_in['b'], 'L1_cond_W': _L1_cond_in['W'], 'L1_cond_b': _L1_cond_in['b'], 'L1_cond_alpha': _L1_cond_in['alpha'], 'L2_cond_W_f': _L2_cond_in['W_f'], 'L2_cond_b_f': _L2_cond_in['b_f'], 'L2_cond_W_i': _L2_cond_in['W_i'], 'L2_cond_b_i': _L2_cond_in['b_i'], 'L2_cond_W_h': _L2_cond_in['W_h'], 'L2_cond_b_h': _L2_cond_in['b_h'], 'L3_cond_base_up': _L3_cond_in['base_up'], 'L3_cond_base_down': _L3_cond_in['base_down'], 'L3_cond_ln_gamma': _L3_cond_in['ln_gamma'], 'L3_cond_ln_beta': _L3_cond_in['ln_beta'], 'L3_cond_W1': _L3_cond_in['W1'], 'L3_cond_bias1': _L3_cond_in['bias1'], 'L3_cond_W2': _L3_cond_in['W2'], 'L3_cond_bias2': _L3_cond_in['bias2']}

def reference(x, cond_1024, L0_cond_W_z, L0_cond_U_z, L0_cond_C_z, L0_cond_b_z, L0_cond_W_r, L0_cond_U_r, L0_cond_C_r, L0_cond_b_r, L0_cond_W, L0_cond_U, L0_cond_C, L0_cond_b, L1_cond_W, L1_cond_b, L1_cond_alpha, L2_cond_W_f, L2_cond_b_f, L2_cond_W_i, L2_cond_b_i, L2_cond_W_h, L2_cond_b_h, L3_cond_base_up, L3_cond_base_down, L3_cond_ln_gamma, L3_cond_ln_beta, L3_cond_W1, L3_cond_bias1, L3_cond_W2, L3_cond_bias2):
    import jax
    import jax.numpy as jnp

    def _L0_cond_ref(video, seq, W_z, U_z, C_z, b_z, W_r, U_r, C_r, b_r, W, U, C, b):
        import jax, jax.numpy as jnp
        import numpy as np
        B, T, D_IN, V_IN, E = (64, 128, 256, 256, 256)
        vz = video @ C_z + b_z
        vr = video @ C_r + b_r
        vh = video @ C + b
        xz = jnp.einsum('btd,de->bte', seq, W_z)
        xr = jnp.einsum('btd,de->bte', seq, W_r)
        xh = jnp.einsum('btd,de->bte', seq, W)

        def step(h, xs):
            xzt, xrt, xht = xs
            z = jax.nn.sigmoid(xzt + h @ U_z + vz)
            r = jax.nn.sigmoid(xrt + h @ U_r + vr)
            hh = jnp.tanh(xht + r * h @ U + vh)
            h_new = (1.0 - z) * h + z * hh
            return (h_new, h_new)
        h0 = jnp.zeros((seq.shape[0], U.shape[0]), seq.dtype)
        xs = (jnp.swapaxes(xz, 0, 1), jnp.swapaxes(xr, 0, 1), jnp.swapaxes(xh, 0, 1))
        _, out_t = jax.lax.scan(step, h0, xs)
        return jnp.swapaxes(out_t, 0, 1)

    def _L1_cond_ref(h_t, z, W, b, alpha):
        import jax, jax.numpy as jnp
        import numpy as np
        LATENT = 256
        D = h_t.shape[-1]
        Wh = W[:, :D]
        Wz = W[:, D:]
        leak = 1.0 - alpha

        def step(h, z_t):
            gate = jax.nn.sigmoid(h @ Wh.T + z_t @ Wz.T + b)
            h_new = jnp.tanh(h * leak + gate * z_t)
            return (h_new, h_new)
        _, hs = jax.lax.scan(step, h_t, jnp.swapaxes(z, 0, 1))
        return jnp.swapaxes(hs, 0, 1)

    def _L2_cond_ref(input_seq, initial_hidden, W_f, b_f, W_i, b_i, W_h, b_h):
        import jax, jax.numpy as jnp
        import numpy as np
        EPS = 1e-08
        forget_gate = jax.nn.sigmoid(jnp.einsum('bsd,hd->bsh', input_seq, W_f) + b_f)
        input_gate = jax.nn.sigmoid(jnp.einsum('bsd,hd->bsh', input_seq, W_i) + b_i)
        gate_sum = forget_gate + input_gate + EPS
        forget_norm = forget_gate / gate_sum
        input_norm = input_gate / gate_sum
        candidate = jnp.einsum('bsd,hd->bsh', input_seq, W_h) + b_h
        new_info = input_norm * candidate
        log_ret = jnp.log(forget_norm + EPS)
        log_cumprod = jnp.cumsum(log_ret, axis=1)
        B, _, H = log_cumprod.shape
        padded = jnp.concatenate([jnp.zeros((B, 1, H), dtype=log_cumprod.dtype), log_cumprod], axis=1)
        scaling = jnp.exp(log_cumprod[:, -1:, :] - padded[:, :-1, :])
        hidden = jnp.cumsum(scaling * new_info, axis=1)
        hidden = hidden + jnp.exp(log_cumprod) * initial_hidden[:, None, :]
        return hidden

    def _L3_cond_ref(x, ada_emb, base_up, base_down, ln_gamma, ln_beta, W1, bias1, W2, bias2):
        import jax, jax.numpy as jnp
        import numpy as np
        RANK = 8
        LN_EPS = 1e-05
        B, T, D = x.shape
        R = RANK
        mu = jnp.mean(ada_emb, axis=-1, keepdims=True)
        var = jnp.mean(jnp.square(ada_emb - mu), axis=-1, keepdims=True)
        c = (ada_emb - mu) / jnp.sqrt(var + LN_EPS) * ln_gamma + ln_beta
        h = jax.nn.gelu(c @ W1 + bias1, approximate=False)
        w = h @ W2 + bias2
        a1, b1, a2, b2 = [t.reshape(B, D, R) for t in jnp.split(w, 4, axis=-1)]
        u = jnp.einsum('btd,bdr->btr', x, a2)
        mid = jnp.einsum('btd,dl->btl', x, base_down) + jnp.einsum('btr,blr->btl', u, b2)
        mid = jax.nn.gelu(mid, approximate=False)
        v = jnp.einsum('blr,btl->btr', b1, mid)
        out = jnp.einsum('btl,kl->btk', mid, base_up) + jnp.einsum('bkr,btr->btk', a1, v)
        return x + out
    x = x + _L0_cond_ref(cond_1024, x, L0_cond_W_z, L0_cond_U_z, L0_cond_C_z, L0_cond_b_z, L0_cond_W_r, L0_cond_U_r, L0_cond_C_r, L0_cond_b_r, L0_cond_W, L0_cond_U, L0_cond_C, L0_cond_b)
    x = x + _L1_cond_ref(cond_1024, x, L1_cond_W, L1_cond_b, L1_cond_alpha)
    x = x + _L2_cond_ref(x, cond_1024, L2_cond_W_f, L2_cond_b_f, L2_cond_W_i, L2_cond_b_i, L2_cond_W_h, L2_cond_b_h)
    x = x + _L3_cond_ref(x, cond_1024, L3_cond_base_up, L3_cond_base_down, L3_cond_ln_gamma, L3_cond_ln_beta, L3_cond_W1, L3_cond_bias1, L3_cond_W2, L3_cond_bias2)
    return x

_drawn_inputs = setup_inputs


def setup_inputs(seed=0):
    import zlib

    import numpy as np

    out = dict(_drawn_inputs(seed))
    spreads = {'L0_cond_b_z': (0.0, 2.0),
     'L0_cond_b_r': (0.0, 2.0),
     'L0_cond_b': (0.0, 0.1),
     'L1_cond_alpha': (0.10000000149011612, 0.6),
     'L2_cond_b_f': (0.0, 2.0),
     'L2_cond_b_i': (0.0, 2.0),
     'L2_cond_b_h': (0.0, 2.0),
     'L3_cond_ln_gamma': (1.0, 0.2),
     'L3_cond_ln_beta': (0.0, 0.1),
     'L3_cond_bias1': (0.0, 0.1),
     'L3_cond_bias2': (0.0, 0.1)}
    factors = {'L0_cond_W_z': 6.018,
     'L0_cond_U_z': 44.35,
     'L0_cond_C_z': 8.0,
     'L0_cond_W_r': 64.0,
     'L0_cond_U_r': 64.0,
     'L0_cond_C_r': 56.228,
     'L1_cond_b': 8.0,
     'L2_cond_W_f': 4.16,
     'L2_cond_W_i': 4.186,
     'L3_cond_base_up': 3.98,
     'L3_cond_base_down': 3.858,
     'L2_cond_W_h': 2.77}
    for name, (base, spread) in spreads.items():
        noise = np.random.default_rng([zlib.crc32(name.encode()), seed]).standard_normal(out[name].shape)
        drawn = base * np.exp(spread * noise) if base else spread * noise
        out[name] = jnp.asarray(drawn.astype(out[name].dtype))
    for name, factor in factors.items():
        out[name] = (out[name] * factor).astype(out[name].dtype)
    return out
```

```python
import concourse.bass as bass
from concourse import mybir
from contextlib import ExitStack

B, T, D, R = 32, 256, 256, 8
P = 128
HALVES, SLABS, BLK = 2, 4, 32
SLAB = D // SLABS
SLOT = 4
BODY = 2 * SLOT
T_PAD = T + BODY
GB = 4
GROUPS = B // GB
COLS = 2 * T
EPS, LN_EPS = 1e-8, 1e-5


def build_program(nc, io):
    fp32, bf16 = mybir.dt.float32, mybir.dt.bfloat16
    ALU, ACT = mybir.AluOpType, mybir.ActivationFunctionType
    ctx = ExitStack()
    with ctx:
        def sb(name, shape, dt=fp32):
            return ctx.enter_context(nc.sbuf_tensor(name, shape, dt))

        def pb(name, shape):
            return ctx.enter_context(nc.psum_tensor(name, shape, fp32))

        def sem(name):
            return ctx.enter_context(nc.semaphore(name))

        wx = sb("wx", [P, HALVES, SLABS, 3, SLAB])
        cx = sb("cx", [P, HALVES, SLABS, 3, SLAB])
        urz = sb("urz", [P, HALVES, SLABS, 2, SLAB])
        uh = sb("uh", [P, HALVES, SLABS, SLAB])
        wz1 = sb("wz1", [P, HALVES, SLABS, SLAB])
        wh1 = sb("wh1", [P, HALVES, SLABS, SLAB])
        bias_rows = sb("bias_rows", [P, 4, SLAB])
        cond_f = sb("cond_f", [P, HALVES, B])
        leak = sb("leak", [P, HALVES, B])
        const_row = sb("const_row", [P, 4, SLAB])
        rest1 = sb("rest1", [P, 4, SLAB])
        rest2 = sb("rest2", [P, 4, SLAB])
        const_parts = [sb(f"const_part{n}", [P, 4, SLAB], bf16) for n in range(3)]
        ident = sb("ident", [P, P], bf16)

        x_in = sb("x_in", [P, 2, SLOT, HALVES, B])
        r_gate = sb("r_gate", [P, 2, SLAB])
        zero_z = sb("zero_z", [P, 2, SLAB, 2])
        cand_kept = sb("cand_kept", [P, 2, SLAB, 2])
        none_h = sb("none_h", [P, 2, SLAB, 2])
        h_f = sb("h_f", [P, 2, HALVES, B])
        x1_f = sb("x1_f", [P, 2, HALVES, B])
        rh = sb("rh", [P, 2, SLAB])
        rh_f = sb("rh_f", [P, 2, HALVES, B])
        zh = sb("zh", [P, 2, SLAB])
        gate = sb("gate", [P, 2, SLAB])
        gate_f = sb("gate_f", [P, 2, HALVES, B])
        gx = sb("gx", [P, 2, HALVES, B])
        leaked = sb("leaked", [P, 2, HALVES, B])
        pre1 = sb("pre1", [P, 2, HALVES, B])
        h1_f = sb("h1_f", [P, 2, HALVES, B])
        x2 = sb("x2", [P, HALVES, B, T])

        wl2 = sb("wl2", [P, HALVES, 3, HALVES, P])
        bl2 = sb("bl2", [P, 3, HALVES])
        wdown = sb("wdown", [P, HALVES, HALVES, P])
        wup = sb("wup", [P, HALVES, HALVES, P])
        w1 = sb("w1", [P, HALVES, HALVES, P])
        bias1 = sb("bias1", [P, HALVES])
        w2 = sb("w2", [P, 2048])
        bias2_f = sb("bias2_f", [P, 2, R, HALVES])
        bias2_b = sb("bias2_b", [P, 2, 512])
        cond_rows = sb("cond_rows", [P, D])
        cond_slab = sb("cond_slab", [P, SLAB])
        gamma = sb("gamma", [P, SLAB])
        beta = sb("beta", [P, SLAB])
        stats = sb("stats", [P, 6])
        mean_var = sb("mean_var", [P, 2])
        var_eps = sb("var_eps", [P, 1])
        std = sb("std", [P, 1])
        rstd = sb("rstd", [P, 1])
        normed = sb("normed", [P, SLAB])
        scaled = sb("scaled", [P, SLAB])
        ada = sb("ada", [P, SLAB])
        ada_f = sb("ada_f", [P, HALVES, B])
        hid_f = sb("hid_f", [P, HALVES, B])
        rank_in = sb("rank_in", [P, 2, HALVES, B, R])
        rank_b = sb("rank_b", [P, 2, 512])
        rank_out = sb("rank_out", [P, 2, GROUPS, D])

        f_t = sb("f_t", [P, 2, COLS])
        i_t = sb("i_t", [P, 2, COLS])
        c_t = sb("c_t", [P, 2, COLS])
        rec = sb("rec", [P, 2, COLS])
        ic = sb("ic", [P, 2, COLS])
        ni = sb("ni", [P, 2, COLS])
        old = [w[:].rearrange("p a b c e -> p (a b c e)")[:, n * COLS:(n + 1) * COLS]
               for w, count in ((wx, 3), (cx, 3), (urz, 2)) for n in range(count)]
        old += [w[:].rearrange("p a b e -> p (a b e)") for w in (uh, wz1, wh1)]
        s_t, fn, fe, wrev, dec, wn, csum, hid2 = old[:8]
        rout_g = [old[8 + n].rearrange("p (w d) -> p w d", w=2) for n in range(2)]
        u_s, v_s = old[10][:, 0:T], old[10][:, T:2 * T]
        x3 = sb("x3", [P, 2, HALVES, GB, T])
        rin_g = sb("rin_g", [P, 2, 2, HALVES, GB, BLK])
        mid = w2[:].rearrange("p (q h t) -> p q h t", q=GB, h=HALVES)
        y = sb("y", [P, 2, HALVES, T])

        banks = [pb(f"bank{n}", [P, 512]) for n in range(8)]
        pre_a = banks[0:2]
        pre_g = banks[2:4]

        weights_in = sem("weights_in")
        tail_in = sem("tail_in")
        w2_in = [sem("w2_in0"), sem("w2_in1")]
        ident_zero, ident_done = sem("ident_zero"), sem("ident_done")
        x_loaded = [sem("x_loaded0"), sem("x_loaded1")]
        const_pre, const_row_done, part_done, rest_done = (
            sem("const_pre"), sem("const_row_done"), sem("part_done"), sem("rest_done"))
        first_pre, first_z, first_cand = (
            sem("first_pre"), sem("first_z"), sem("first_cand"))
        zero_done = sem("zero_done")
        leak_done = sem("leak_done")
        rz_pre, cand_pre, gate_pre = sem("rz_pre"), sem("cand_pre"), sem("gate_pre")
        r_done, z_done, cand_done, gate_done, h1_done = sem("r_done"), sem("z_done"), sem("cand_done"), sem("gate_done"), sem("h1_done")
        rh_done, rhf_done, zh_done, kept_done = sem("rh_done"), sem("rhf_done"), sem("zh_done"), sem("kept_done")
        gatef_done, gx_done, pre1_done = sem("gatef_done"), sem("gx_done"), sem("pre1_done")
        h_done, hf_done, x1_done = sem("h_done"), sem("hf_done"), sem("x1_done")
        leaked_done, x2_done = sem("leaked_done"), sem("x2_done")

        ln_step, std_done, ada_done, hid_pre, hid_done = (
            sem("ln_step"), sem("std_done"), sem("ada_done"), sem("hid_pre"), sem("hid_done"))
        w2_used, rin_done, rb_done = (
            sem("w2_used"), sem("rin_done"), sem("rb_done"))
        scratch_out, rout_in = sem("scratch_out"), sem("rout_in")
        pad_done = sem("pad_done")

        l2_pre, f_done, i_done, c_done = sem("l2_pre"), sem("f_done"), sem("i_done"), sem("c_done")
        s_done, rec_done, fn_done, fe_done, ic_done, ni_done = (
            sem("s_done"), sem("rec_done"), sem("fn_done"), sem("fe_done"), sem("ic_done"), sem("ni_done"))
        wrev_done, wn_done, csum_done, dec_done, hid2_done, x3_done = (
            sem("wrev_done"), sem("wn_done"), sem("csum_done"), sem("dec_done"), sem("hid2_done"), sem("x3_done"))
        stage_done = sem("stage_done")
        u_pre, u_done, mid_pre, mid_done, v_pre, v_done, out_pre, y_done = (
            sem("u_pre"), sem("u_done"), sem("mid_pre"), sem("mid_done"), sem("v_pre"), sem("v_done"),
            sem("out_pre"), sem("y_done"))
        y_stored = [sem("y_stored0"), sem("y_stored1")]

        WEIGHT_LOADS = [(wx, "wx"), (cx, "cx"), (bias_rows, "bias_rows"), (cond_f, "cond_f"), (urz, "urz"),
                        (uh, "uh"), (wz1, "wz1"), (wh1, "wh1"), (leak, "alpha")]
        TAIL_LOADS = [(cond_rows, "cond_rows"), (cond_slab, "cond_slab"), (gamma, "gamma"), (beta, "beta"),
                      (w1, "w1"), (bias1, "bias1"), (bias2_f, "bias2_f"), (bias2_b, "bias2_b"),
                      (wl2, "wl2"), (bl2, "bl2"), (wdown, "wdown"), (wup, "wup")]
        W2_PIECES = 8
        STAGED = 4
        scratch = io["scratch"]

        block = ctx.enter_context(nc.Block())

        @block.sync
        def _(sp):
            for dst, name in WEIGHT_LOADS:
                sp.dma_start(dst[:], io[name]).then_inc(weights_in, 16)
            for s in range(2):
                sp.dma_start(x_in[:, s], io["x"][:, s * SLOT:(s + 1) * SLOT]).then_inc(x_loaded[s], 16)
            for dst, name in TAIL_LOADS:
                sp.dma_start(dst[:], io[name]).then_inc(tail_in, 16)
            with sp.Fori(0, T // BODY) as n:
                for s in range(2):
                    sp.wait_ge(x1_done, n * BODY + (s + 1) * SLOT)
                    sp.dma_start(x_in[:, s], io["x"][:, bass.ds(n * BODY + BODY + s * SLOT, SLOT)]
                                 ).then_inc(x_loaded[s], 16)

            for k in range(W2_PIECES):
                if k >= 2:
                    sp.wait_ge(w2_used, k - 1)
                half = (k % 2) * 1024
                sp.dma_start(w2[:, half:half + 1024].rearrange("p (h n) -> p h n", h=HALVES),
                             io["w2"][:, :, k * 512:(k + 1) * 512]).then_inc(w2_in[k % 2], 16)
            for k in range(W2_PIECES):
                sp.wait_ge(w2_used, W2_PIECES + k - 1)
                half = (k % 2) * 1024
                sp.dma_start(w2[:, half:half + 1024].rearrange("p (h n) -> p h n", h=HALVES),
                             io["w2"][:, :, 4096 + k * 512:4096 + (k + 1) * 512]
                             ).then_inc(w2_in[k % 2], 16)
            sp.wait_ge(rb_done, 2)
            for q in range(SLABS):
                for w in range(2):
                    sp.dma_start(scratch[w, :, 2 * q:2 * q + 2, :].rearrange("b r d -> b (r d)"),
                                 rank_b[32 * q:32 * q + 32, w, :]).then_inc(scratch_out, 16)
            sp.wait_ge(scratch_out, 16 * 2 * SLABS)
            sp.wait_ge(pad_done, 2)
            for q in range(GB):
                for w in range(2):
                    sp.dma_start(rank_out[32 * q:32 * q + R, w],
                                 scratch[w].rearrange("(g q) r d -> q r g d", q=GB)[q]).then_inc(rout_in, 16)

            sp.sem_inc(y_stored[0], 1)
            sp.sem_inc(y_stored[1], 1)
            with sp.Fori(0, GROUPS) as g:
                for q in range(GB):
                    sp.wait_ge(y_done, g * GB + q + 2)
                    sp.dma_start(io["out"][:, :, bass.ds(g * GB + q, 1), :].rearrange("p h o t -> p h (o t)"),
                                 y[:, q % 2]).then_inc(y_stored[q % 2], 16)
            for s in range(2):
                sp.wait_ge(y_stored[s], 16 * B // 2 + 1)

        @block.gpsimd
        def _(pool):
            pool.memset(ident[:], 0.0).then_inc(ident_zero, 1)
            pool.wait_ge(ident_zero, 1)
            pool.affine_select(out=ident[:], in_=ident[:], compare_op=ALU.not_equal, fill=1.0, base=0,
                               pattern=[[-1, P]], channel_multiplier=1).then_inc(ident_done, 1)
            pool.memset(rin_g[:], 0.0).then_inc(pad_done, 1)
            pool.memset(rank_out[:], 0.0).then_inc(pad_done, 1)
            pool.sem_inc(x2_done, 1)
            pool.sem_inc(y_done, 1)
            pool.wait_ge(leak_done, 1)
            pool.tensor_tensor(leaked[:, 0], leak[:], cond_f[:], ALU.mult).then_inc(leaked_done, 1)
            with pool.Fori(0, T // BODY) as n:
                for u in range(BODY):
                    t = n * BODY + u
                    pool.wait_ge(h1_done, t + 2)
                    pool.tensor_tensor(leaked[:, (u + 1) % 2], leak[:], h1_f[:, u % 2],
                                       ALU.mult).then_inc(leaked_done, 1)
                    pool.tensor_tensor(x2[:, :, :, t], x1_f[:, u % 2], h1_f[:, u % 2],
                                       ALU.add).then_inc(x2_done, 1)
            pool.wait_ge(pad_done, 2)

            def new_info(p, units):
                for unit in units:
                    k, c = unit % 2, p * 4 + unit
                    pool.wait_ge(c_done, c + 1)
                    pool.tensor_tensor(ic[:, k], i_t[:, k], c_t[:, k], ALU.mult).then_inc(ic_done, 1)
                    pool.wait_ge(rec_done, c + 1)
                    pool.wait_ge(ic_done, c + 1)
                    pool.tensor_tensor(ni[:, k], ic[:, k], rec[:, k], ALU.mult).then_inc(ni_done, 1)

            def factors(g, par):
                for w in range(2):
                    pool.tensor_copy(rin_g[:, par, w, :, :, 0:R], rank_in[:, w, :, bass.ds(g * GB, GB), :]
                                     ).then_inc(stage_done, 1)
                    pool.tensor_copy(rout_g[par][:, w, :], rank_out[:, w, bass.ds(g, 1), :]
                                     .rearrange("p o d -> p (o d)")).then_inc(stage_done, 1)

            def phase(p, par):
                new_info(p, range(2))
                pool.wait_ge(y_done, p * GB - GB + 1)
                factors(p, par)
                new_info(p, range(2, 4))

            new_info(0, range(4))
            pool.wait_ge(rin_done, 4)
            pool.wait_ge(rout_in, 16 * 2 * GB)
            factors(0, 0)
            new_info(1, range(2))
            factors(1, 1)
            new_info(1, range(2, 4))
            with pool.Fori(0, (GROUPS - 2) // 2) as n:
                phase(2 * n + 2, 0)
                phase(2 * n + 3, 1)

        @block.scalar
        def _(act):
            act.wait_ge(first_pre, 1)
            act.wait_ge(zero_done, 1)
            act.activation(zero_z[:, 0, :, 1], pre_a[0][:, SLAB:2 * SLAB], ACT.Sigmoid).then_inc(first_z, 1)
            act.activation(cand_kept[:, 0, :, 0], pre_a[0][:, 2 * SLAB:3 * SLAB], ACT.Tanh).then_inc(first_cand, 1)
            with act.Fori(0, T // BODY) as n:
                for u in range(BODY):
                    t, now, nxt = n * BODY + u, u % 2, (u + 1) % 2
                    act.wait_ge(rz_pre, t + 1)
                    act.activation(r_gate[:, nxt], pre_a[nxt][:, 0:SLAB], ACT.Sigmoid).then_inc(r_done, 1)
                    act.activation(zero_z[:, nxt, :, 1], pre_a[nxt][:, SLAB:2 * SLAB],
                                   ACT.Sigmoid).then_inc(z_done, 1)
                    act.wait_ge(gate_pre, t + 1)
                    act.activation(gate[:, now], pre_g[now][:, 0:SLAB], ACT.Sigmoid).then_inc(gate_done, 1)
                    act.wait_ge(cand_pre, t + 1)
                    act.activation(cand_kept[:, nxt, :, 0], pre_a[nxt][:, 2 * SLAB:3 * SLAB],
                                   ACT.Tanh).then_inc(cand_done, 1)
                    act.wait_ge(pre1_done, t + 1)
                    act.activation(h1_f[:, now], pre1[:, now], ACT.Tanh).then_inc(h1_done, 1)

            def gates(p, units, first=False):
                for unit in units:
                    k, c, m = unit % 2, p * 4 + unit, unit % 2
                    for mat, (dst, fun, done) in enumerate(
                            ((f_t, ACT.Sigmoid, f_done), (i_t, ACT.Sigmoid, i_done), (c_t, ACT.Identity, c_done))):
                        act.wait_ge(l2_pre, p * 12 + unit * 3 + mat + 1)
                        if mat == 0 and not (first and unit < 2):
                            act.wait_ge(fn_done, c - 1)
                            act.wait_ge(ic_done, c - 1)
                        act.activation(dst[:, k], banks[(unit * 3 + mat) % 4][:], fun,
                                       bias=bl2[:, mat, m:m + 1]).then_inc(done, 1)

            def hidden_layer(g):
                act.wait_ge(u_pre, g + 1)
                act.activation(u_s, banks[4][:, 0:T], ACT.Copy).then_inc(u_done, 1)
                for q in range(GB):
                    act.wait_ge(mid_pre, g * GB + q + 1)
                    act.activation(mid[:, q].rearrange("p h t -> p (h t)"), banks[5 + q % 3][:],
                                   ACT.Gelu).then_inc(mid_done, 1)

            def ranks_out(g):
                act.wait_ge(v_pre, g + 1)
                act.activation(v_s, banks[4][:, 0:T], ACT.Copy).then_inc(v_done, 1)

            act.wait_ge(ln_step, 3)
            act.activation(std[:], var_eps[:], ACT.Sqrt).then_inc(std_done, 1)
            gates(0, range(2), first=True)
            act.wait_ge(hid_pre, 1)
            for m in range(HALVES):
                act.activation(hid_f[:, m], banks[4][:, m * B:(m + 1) * B], ACT.Gelu,
                               bias=bias1[:, m:m + 1]).then_inc(hid_done, 1)
            gates(0, range(2, 4))
            with act.Fori(0, GROUPS - 1) as n:
                gates(n + 1, range(2))
                hidden_layer(n)
                gates(n + 1, range(2, 3))
                ranks_out(n)
                gates(n + 1, range(3, 4))
            hidden_layer(GROUPS - 1)
            ranks_out(GROUPS - 1)

        @block.vector
        def _(dve):
            dve.wait_ge(weights_in, 16 * len(WEIGHT_LOADS))
            dve.memset(zero_z[:], 0.0).then_inc(zero_done, 1)
            dve.tensor_scalar(leak[:], leak[:], -1.0, 1.0, ALU.mult, ALU.add).then_inc(leak_done, 1)
            dve.tensor_copy(h1_f[:, 1], cond_f[:]).then_inc(h1_done, 1)
            dve.wait_ge(const_pre, 1)
            dve.tensor_tensor(const_row[:, 0:3].rearrange("p a e -> p (a e)"), pre_a[0][:, 0:192],
                              bias_rows[:, 0:3].rearrange("p a e -> p (a e)"), ALU.add).then_inc(const_row_done, 1)
            dve.tensor_copy(const_row[:, 3], bias_rows[:, 3]).then_inc(const_row_done, 1)
            dve.wait_ge(const_row_done, 2)
            dve.tensor_copy(const_parts[0][:], const_row[:]).then_inc(part_done, 1)
            dve.wait_ge(part_done, 1)
            dve.tensor_tensor(rest1[:], const_row[:], const_parts[0][:], ALU.subtract).then_inc(rest_done, 1)
            dve.wait_ge(rest_done, 1)
            dve.tensor_copy(const_parts[1][:], rest1[:]).then_inc(part_done, 1)
            dve.wait_ge(part_done, 2)
            dve.tensor_tensor(rest2[:], rest1[:], const_parts[1][:], ALU.subtract).then_inc(rest_done, 1)
            dve.wait_ge(rest_done, 2)
            dve.tensor_copy(const_parts[2][:], rest2[:]).then_inc(part_done, 1)
            dve.wait_ge(first_cand, 1)
            dve.tensor_tensor(none_h[:, 0, :, 1], zero_z[:, 0, :, 1], cand_kept[:, 0, :, 0],
                              ALU.mult).then_inc(h_done, 1)
            dve.wait_ge(h_done, 1)
            dve.transpose(h_f[:, 0].rearrange("p h b -> p (h b)"), none_h[:, 0, :, 1]).then_inc(hf_done, 1)
            dve.wait_ge(x_loaded[0], 16)
            dve.wait_ge(hf_done, 1)
            dve.tensor_tensor(x1_f[:, 0], x_in[:, 0, 0], h_f[:, 0], ALU.add).then_inc(x1_done, 1)

            with dve.Fori(0, T // BODY) as n:
                for u in range(BODY):
                    t, now, nxt = n * BODY + u, u % 2, (u + 1) % 2
                    slot, at = ((u + 1) // SLOT) % 2, (u + 1) % SLOT
                    dve.wait_ge(r_done, t + 1)
                    dve.tensor_tensor(rh[:, nxt], r_gate[:, nxt], none_h[:, now, :, 1], ALU.mult).then_inc(rh_done, 1)
                    dve.wait_ge(rh_done, t + 1)
                    dve.transpose(rh_f[:, nxt].rearrange("p h b -> p (h b)"), rh[:, nxt]).then_inc(rhf_done, 1)
                    dve.wait_ge(z_done, t + 1)
                    dve.tensor_tensor(zh[:, nxt], zero_z[:, nxt, :, 1], none_h[:, now, :, 1],
                                      ALU.mult).then_inc(zh_done, 1)
                    dve.wait_ge(zh_done, t + 1)
                    dve.tensor_tensor(cand_kept[:, nxt, :, 1], none_h[:, now, :, 1], zh[:, nxt],
                                      ALU.subtract).then_inc(kept_done, 1)
                    dve.wait_ge(gate_done, t + 1)
                    dve.transpose(gate_f[:, now].rearrange("p h b -> p (h b)"), gate[:, now]).then_inc(gatef_done, 1)
                    dve.wait_ge(gatef_done, t + 1)
                    dve.tensor_tensor(gx[:, now], gate_f[:, now], x1_f[:, now], ALU.mult).then_inc(gx_done, 1)
                    dve.wait_ge(cand_done, t + 1)
                    dve.wait_ge(kept_done, t + 1)
                    dve.tensor_tensor_scan(none_h[:, nxt].rearrange("p e a -> p (e a)"),
                                           zero_z[:, nxt].rearrange("p e a -> p (e a)"),
                                           cand_kept[:, nxt].rearrange("p e a -> p (e a)"),
                                           0.0, ALU.mult, ALU.add).then_inc(h_done, 1)
                    dve.wait_ge(gx_done, t + 1)
                    dve.wait_ge(leaked_done, t + 1)
                    dve.tensor_tensor(pre1[:, now], gx[:, now], leaked[:, now], ALU.add).then_inc(pre1_done, 1)
                    dve.wait_ge(h_done, t + 2)
                    dve.transpose(h_f[:, nxt].rearrange("p h b -> p (h b)"), none_h[:, nxt, :, 1]).then_inc(hf_done, 1)
                    if at == 0:
                        dve.wait_ge(x_loaded[slot], (n + 1 + (1 if slot == 0 else 0)) * 16)
                    dve.wait_ge(x2_done, t + 1)
                    dve.wait_ge(hf_done, t + 2)
                    dve.tensor_tensor(x1_f[:, nxt], x_in[:, slot, at], h_f[:, nxt], ALU.add).then_inc(x1_done, 1)

            dve.wait_ge(tail_in, 16 * len(TAIL_LOADS))
            dve.bn_stats(stats[:], cond_rows[:]).then_inc(ln_step, 1)
            dve.wait_ge(ln_step, 1)
            dve.bn_aggr(mean_var[:], stats[:]).then_inc(ln_step, 1)
            dve.wait_ge(ln_step, 2)
            dve.tensor_scalar(var_eps[:], mean_var[:, 1:2], LN_EPS, None, ALU.add).then_inc(ln_step, 1)
            dve.wait_ge(std_done, 1)
            dve.reciprocal(rstd[:], std[:]).then_inc(ln_step, 1)
            dve.wait_ge(ln_step, 4)
            dve.tensor_scalar(normed[:], cond_slab[:], mean_var[:, 0:1], rstd[:, 0:1],
                              ALU.subtract, ALU.mult).then_inc(ln_step, 1)
            dve.wait_ge(ln_step, 5)
            dve.tensor_tensor(scaled[:], normed[:], gamma[:], ALU.mult).then_inc(ln_step, 1)
            dve.wait_ge(ln_step, 6)
            dve.tensor_tensor(ada[:], scaled[:], beta[:], ALU.add).then_inc(ln_step, 1)
            dve.wait_ge(ln_step, 7)
            dve.transpose(ada_f[:].rearrange("p h b -> p (h b)"), ada[:]).then_inc(ada_done, 1)

            def scan_unit(p, unit, par):
                k, c, m, hf = unit % 2, p * 4 + unit, unit % 2, unit // 2
                dve.wait_ge(i_done, c + 1)
                dve.scalar_tensor_tensor(s_t, f_t[:, k], EPS, i_t[:, k], ALU.add, ALU.add).then_inc(s_done, 1)
                dve.wait_ge(s_done, c + 1)
                dve.reciprocal(rec[:, k], s_t).then_inc(rec_done, 1)
                dve.wait_ge(rec_done, c + 1)
                dve.tensor_tensor(fn, f_t[:, k], rec[:, k], ALU.mult).then_inc(fn_done, 1)
                dve.wait_ge(fn_done, c + 1)
                dve.tensor_scalar(fe, fn, EPS, None, ALU.add).then_inc(fe_done, 1)
                dve.wait_ge(fe_done, c + 1)
                for b in range(2):
                    rev = slice(b * T, (b + 1) * T)
                    dve.tensor_tensor_scan(wrev[:, rev][:, ::-1], fe[:, rev][:, ::-1], fe[:, rev][:, ::-1],
                                           1.0, ALU.mult, ALU.bypass).then_inc(wrev_done, 1)
                for b in range(2):
                    col = slice(b * T, (b + 1) * T)
                    dve.tensor_tensor_scan(dec[:, col], fe[:, col], fe[:, col],
                                           cond_f[:, m, bass.ds(p * GB + 2 * hf + b, 1)],
                                           ALU.mult, ALU.bypass).then_inc(dec_done, 1)
                dve.wait_ge(wrev_done, 2 * c + 2)
                dve.wait_ge(ni_done, c + 1)
                dve.tensor_tensor(wn, wrev, ni[:, k], ALU.mult).then_inc(wn_done, 1)
                dve.wait_ge(wn_done, c + 1)
                for b in range(2):
                    col = slice(b * T, (b + 1) * T)
                    dve.tensor_tensor_scan(csum[:, col], wn[:, col], wn[:, col],
                                           0.0, ALU.add, ALU.bypass).then_inc(csum_done, 1)
                dve.wait_ge(csum_done, 2 * c + 2)
                dve.wait_ge(dec_done, 2 * c + 2)
                dve.tensor_tensor(hid2, csum, dec, ALU.add).then_inc(hid2_done, 1)
                dve.wait_ge(hid2_done, c + 1)
                dve.tensor_tensor(x3[:, par, m, 2 * hf:2 * hf + 2, :].rearrange("p q t -> p (q t)"),
                                  x2[:, m, bass.ds(p * GB + 2 * hf, 2), :].rearrange("p q t -> p (q t)"),
                                  hid2, ALU.add).then_inc(x3_done, 1)

            def outputs(g, qs, par):
                for q in qs:
                    dve.wait_ge(out_pre, g * GB + q + 1)
                    dve.wait_ge(y_stored[q % 2], (g * 2 + q // 2) * 16 + 1)
                    dve.scalar_tensor_tensor(y[:, q % 2], x3[:, par, :, q, :], 2.0,
                                             banks[5 + (GB + q) % 3][:].rearrange("p (h t) -> p h t", h=HALVES),
                                             ALU.mult, ALU.add).then_inc(y_done, 1)

            def phase(p, par):
                for unit in range(3):
                    scan_unit(p, unit, par)
                outputs(p - 1, range(2), 1 - par)
                scan_unit(p, 3, par)
                outputs(p - 1, range(2, 4), 1 - par)

            for unit in range(4):
                scan_unit(0, unit, 0)
            dve.wait_ge(w2_used, W2_PIECES)
            for w in range(2):
                for m in range(HALVES):
                    src = banks[4 + w][:].rearrange("p (r m b) -> p m b r", r=R, m=HALVES)[:, m]
                    bias = bias2_f[:, w, :, m].rearrange("p (o r) -> p o r", o=1).broadcast_to([P, B, R])
                    dve.tensor_tensor(rank_in[:, w, m], src, bias, ALU.add).then_inc(rin_done, 1)
            dve.wait_ge(w2_used, 2 * W2_PIECES)
            for w in range(2):
                dve.tensor_tensor(rank_b[:, w], banks[6 + w][:], bias2_b[:, w], ALU.add).then_inc(rb_done, 1)
            with dve.Fori(0, (GROUPS - 2) // 2) as n:
                phase(2 * n + 1, 1)
                phase(2 * n + 2, 0)
            phase(GROUPS - 1, 1)
            outputs(GROUPS - 1, range(GB), 1)

        @block.tensor
        def _(pe):
            def tiles(out, lo, n, stationary, moving, start=False):
                for k in range(HALVES):
                    for j in range(SLABS):
                        mm = pe.matmul(out[32 * j:32 * j + 32, lo:lo + n], stationary[:, k, :], moving(k, j),
                                       start=start and k == 0, stop=k == 1, tile_position=(0, 32 * j),
                                       skip_group_check=True)
                return mm

            def constants(out, lo, n):
                for part in range(3):
                    mm = pe.matmul(out[:, 0:n], ident[:],
                                   const_parts[part][:].rearrange("p a e -> p (a e)")[:, lo:lo + n],
                                   start=part == 0, stop=False, skip_group_check=True)
                return mm

            flat3 = lambda w: (lambda k, j: w[:, k, j].rearrange("p a e -> p (a e)"))
            flat1 = lambda w: (lambda k, j: w[:, k, j])

            pe.wait_ge(weights_in, 16 * len(WEIGHT_LOADS))
            tiles(pre_a[0], 0, 3 * SLAB, cond_f, flat3(cx), start=True).then_inc(const_pre, 1)
            pe.wait_ge(part_done, 3)
            pe.wait_ge(ident_done, 1)
            pe.wait_ge(x_loaded[0], 16)
            constants(pre_a[0], 0, 3 * SLAB)
            tiles(pre_a[0], 0, 3 * SLAB, x_in[:, 0, 0], flat3(wx)).then_inc(first_pre, 1)

            with pe.Fori(0, T // BODY) as n:
                for u in range(BODY):
                    t, now, nxt = n * BODY + u, u % 2, (u + 1) % 2
                    slot, at = ((u + 1) // SLOT) % 2, (u + 1) % SLOT
                    if at == 0:
                        pe.wait_ge(x_loaded[slot], (n + 1 + (1 if slot == 0 else 0)) * 16)
                    constants(pre_a[nxt], 0, 3 * SLAB)
                    tiles(pre_a[nxt], 0, 3 * SLAB, x_in[:, slot, at], flat3(wx))
                    pe.wait_ge(hf_done, t + 1)
                    tiles(pre_a[nxt], 0, 2 * SLAB, h_f[:, now], flat3(urz)).then_inc(rz_pre, 1)
                    constants(pre_g[now], 3 * SLAB, SLAB)
                    pe.wait_ge(x1_done, t + 1)
                    tiles(pre_g[now], 0, SLAB, x1_f[:, now], flat1(wz1))
                    pe.wait_ge(h1_done, t + 1)
                    tiles(pre_g[now], 0, SLAB, h1_f[:, nxt], flat1(wh1)).then_inc(gate_pre, 1)
                    pe.wait_ge(rhf_done, t + 1)
                    pe.wait_ge(z_done, t + 1)
                    tiles(pre_a[nxt], 2 * SLAB, SLAB, rh_f[:, nxt], flat1(uh)).then_inc(cand_pre, 1)

            def gate_products(p, unit, first=False):
                m, hf = unit % 2, unit // 2
                for mat in range(3):
                    at = unit * 3 + mat
                    if at >= 4 or not first:
                        prev = at - 4 if at >= 4 else at + 8
                        unit_before = (p if at >= 4 else p - 1) * 4 + prev // 3
                        pe.wait_ge((f_done, i_done, c_done)[prev % 3], unit_before + 1)
                    for k in range(HALVES):
                        mm = pe.matmul(banks[at % 4][:], wl2[:, k, mat, m],
                                       x2[:, k, bass.ds(p * GB + 2 * hf, 2), :].rearrange("p q t -> p (q t)"),
                                       start=k == 0, stop=k == 1)
                    mm.then_inc(l2_pre, 1)

            def rank_products(par, w, moving, done):
                for k in range(HALVES):
                    for q in range(GB):
                        mm = pe.matmul(banks[4][32 * q:32 * q + 32, 0:T], rin_g[:, par, w, k, q], moving(k, q),
                                       start=k == 0, stop=k == 1, tile_position=(0, 32 * q))
                mm.then_inc(done, 1)

            def dense(par, q, bank, weights, moving, w, low):
                for m in range(HALVES):
                    for k in range(HALVES):
                        pe.matmul(banks[bank][:, m * T:(m + 1) * T], weights[:, k, m], moving(k, q),
                                  start=k == 0, stop=False, skip_group_check=True)
                    mm = pe.matmul(banks[bank][:, m * T:(m + 1) * T],
                                   rout_g[par][32 * q:32 * q + R, w, m * P:(m + 1) * P],
                                   low[32 * q:32 * q + R, :], start=False, stop=True,
                                   tile_position=(32 * q, 0), skip_group_check=True)
                return mm

            def down(g, par):
                pe.wait_ge(x3_done, g * 4 + 4)
                pe.wait_ge(stage_done, g * STAGED + STAGED)
                rank_products(par, 0, lambda k, q: x3[:, par, k, q], u_pre)
                pe.wait_ge(y_done, g * GB + 1)
                pe.wait_ge(u_done, g + 1)
                for q in range(GB):
                    if q == 3:
                        pe.wait_ge(mid_done, g * GB + 1)
                    dense(par, q, 5 + q % 3, wdown, lambda k, q: x3[:, par, k, q], 1, u_s).then_inc(mid_pre, 1)

            def up_ranks(g, par):
                pe.wait_ge(mid_done, g * GB + GB)
                rank_products(par, 1, lambda k, q: mid[:, q, k], v_pre)

            def up(g, par, qs):
                pe.wait_ge(v_done, g + 1)
                for q in qs:
                    if q == 3:
                        pe.wait_ge(y_done, g * GB + 2)
                    dense(par, q, 5 + (GB + q) % 3, wup, lambda k, q: mid[:, q, k], 0, v_s).then_inc(out_pre, 1)

            def phase(p, par):
                gate_products(p, 0)
                gate_products(p, 1)
                down(p - 1, 1 - par)
                gate_products(p, 2)
                up_ranks(p - 1, 1 - par)
                up(p - 1, 1 - par, range(2))
                gate_products(p, 3)
                up(p - 1, 1 - par, range(2, GB))

            pe.wait_ge(x2_done, T + 1)
            pe.wait_ge(cand_done, T)
            pe.wait_ge(gate_done, T)
            pe.wait_ge(tail_in, 16 * len(TAIL_LOADS))
            gate_products(0, 0, first=True)
            gate_products(0, 1, first=True)
            pe.wait_ge(ada_done, 1)
            for m in range(HALVES):
                for k in range(HALVES):
                    mm = pe.matmul(banks[4][:, m * B:(m + 1) * B], w1[:, k, m], ada_f[:, k],
                                   start=k == 0, stop=k == 1)
            mm.then_inc(hid_pre, 1)
            gate_products(0, 2, first=True)
            gate_products(0, 3, first=True)
            pe.wait_ge(hid_done, 2)
            for piece in range(W2_PIECES):
                pe.wait_ge(w2_in[piece % 2], 16 * (piece // 2 + 1))
                half = (piece % 2) * 1024
                for tile in range(4):
                    at = piece * 4 + tile
                    for k in range(HALVES):
                        col = half + k * 512 + tile * P
                        mm = pe.matmul(banks[4 + at // 16][:, (at % 16) * B:(at % 16 + 1) * B], w2[:, col:col + P],
                                       hid_f[:, k], start=k == 0, stop=k == 1)
                mm.then_inc(w2_used, 1)
            for piece in range(W2_PIECES):
                pe.wait_ge(w2_in[piece % 2], 16 * ((W2_PIECES + piece) // 2 + 1))
                half = (piece % 2) * 1024
                w, q = piece // 4, piece % 4
                for k in range(HALVES):
                    mm = pe.matmul(banks[6 + w][32 * q:32 * q + 32, :], hid_f[:, k],
                                   w2[:, half + k * 512:half + (k + 1) * 512],
                                   start=k == 0, stop=k == 1, tile_position=(0, 32 * q))
                mm.then_inc(w2_used, 1)
            pe.wait_ge(rin_done, 4)
            pe.wait_ge(rb_done, 2)
            with pe.Fori(0, (GROUPS - 2) // 2) as n:
                phase(2 * n + 1, 1)
                phase(2 * n + 2, 0)
            phase(GROUPS - 1, 1)
            down(GROUPS - 1, 1)
            up_ranks(GROUPS - 1, 1)
            up(GROUPS - 1, 1, range(GB))


def _rows(w):
    n = w.shape[1]
    return w.reshape(SLABS, HALVES, BLK, n).transpose(0, 2, 1, 3).reshape(P, HALVES, n)


def _cols(w):
    s = w.shape[:-1]
    w = w.reshape(*s, SLABS, HALVES, BLK)
    n = len(s)
    return w.transpose(*range(n), n + 1, n, n + 2).reshape(*s, HALVES, P)


def _slabs(np, ws):
    return np.stack([_rows(w).reshape(P, HALVES, SLABS, SLAB) for w in ws], axis=3)


def _part(v):
    return v.reshape(SLABS, HALVES, BLK).transpose(0, 2, 1).reshape(P, HALVES)


def kernel(**inputs):
    import numpy as np
    import concourse.bacc as bacc
    from concourse.bass_utils import run_bass_kernel_spmd

    a = {k: np.asarray(v) for k, v in inputs.items()}
    cond = a["cond_1024"]
    slab_rows = lambda v: np.repeat(v.reshape(SLABS, 1, SLAB), B, axis=1).reshape(P, SLAB)
    x = a["x"].reshape(B, T, SLABS, HALVES, BLK).transpose(2, 4, 1, 3, 0).reshape(P, T, HALVES, B)
    x_pad = np.zeros((P, T_PAD, HALVES, B), x.dtype)
    x_pad[:, :T] = x
    w2 = _rows(a["L3_cond_W2"]).reshape(P, HALVES, 4, D, R)
    w2 = _cols(w2.transpose(0, 1, 2, 4, 3))
    w2 = w2[:, :, [2, 1, 0, 3]].reshape(P, HALVES, 4 * R * D)
    b2 = _cols(a["L3_cond_bias2"].reshape(4, D, R).transpose(0, 2, 1))
    host = {
        "x": x_pad,
        "wx": _slabs(np, [a["L0_cond_W_r"], a["L0_cond_W_z"], a["L0_cond_W"]]),
        "cx": _slabs(np, [a["L0_cond_C_r"], a["L0_cond_C_z"], a["L0_cond_C"]]),
        "urz": _slabs(np, [a["L0_cond_U_r"], a["L0_cond_U_z"]]),
        "uh": _slabs(np, [a["L0_cond_U"]])[:, :, :, 0],
        "wz1": _slabs(np, [a["L1_cond_W"][:, D:].T])[:, :, :, 0],
        "wh1": _slabs(np, [a["L1_cond_W"][:, :D].T])[:, :, :, 0],
        "bias_rows": np.stack([slab_rows(a[k]) for k in ("L0_cond_b_r", "L0_cond_b_z", "L0_cond_b", "L1_cond_b")],
                              axis=1),
        "cond_f": _rows(cond.T),
        "alpha": np.repeat(_part(a["L1_cond_alpha"])[:, :, None], B, axis=2),
        "wl2": np.stack([_cols(_rows(a[k].T)) for k in ("L2_cond_W_f", "L2_cond_W_i", "L2_cond_W_h")], axis=2),
        "bl2": np.stack([_part(a[k]) for k in ("L2_cond_b_f", "L2_cond_b_i", "L2_cond_b_h")], axis=1),
        "wdown": _cols(_rows(a["L3_cond_base_down"])),
        "wup": _cols(_rows(a["L3_cond_base_up"].T)),
        "w1": _cols(_rows(a["L3_cond_W1"])),
        "bias1": _part(a["L3_cond_bias1"]),
        "w2": w2,
        "bias2_f": b2[[2, 1]].transpose(3, 0, 1, 2),
        "bias2_b": np.repeat(b2[[0, 3]].reshape(2, SLABS, 1, 512).transpose(1, 2, 0, 3), B, axis=1).reshape(P, 2, 512),
        "cond_rows": np.concatenate([cond] * SLABS, axis=0),
        "cond_slab": cond.reshape(B, SLABS, SLAB).transpose(1, 0, 2).reshape(P, SLAB),
        "gamma": slab_rows(a["L3_cond_ln_gamma"]),
        "beta": slab_rows(a["L3_cond_ln_beta"]),
    }
    nc = bacc.Bacc("TRN2", target_bir_lowering=False, num_devices=1)
    arrays, io = {}, {}
    for name, v in host.items():
        v = np.ascontiguousarray(v)
        arrays[f"in_{name}"] = v
        io[name] = nc.dram_tensor(f"in_{name}", v.shape, mybir.dt.from_np(v.dtype), kind="ExternalInput").ap()
    io["scratch"] = nc.dram_tensor("scratch", (2, B, R, D), mybir.dt.float32, kind="Internal").ap()
    io["out"] = nc.dram_tensor("out_0", (P, HALVES, B, T), mybir.dt.float32, kind="ExternalOutput").ap()
    build_program(nc, io)
    r = run_bass_kernel_spmd(nc, [arrays], core_ids=[0])
    y = r.results[0]["out_0"]
    return y.reshape(SLABS, BLK, HALVES, B, T).transpose(3, 4, 0, 2, 1).reshape(B, T, D)
```

```python
import concourse.bass as bass
from concourse import mybir
from contextlib import ExitStack

B, T, D, R = 32, 256, 256, 8
P = 128
HALVES, SLABS, BLK = 2, 4, 32
SLAB = D // SLABS
SLOT = 8
BODY = 2 * SLOT
T_PAD = T + BODY
GB = 4
GROUPS = B // GB
COLS = 2 * T
EPS, LN_EPS = 1e-8, 1e-5


def build_program(nc, io):
    fp32, bf16 = mybir.dt.float32, mybir.dt.bfloat16
    ALU, ACT = mybir.AluOpType, mybir.ActivationFunctionType
    ctx = ExitStack()
    with ctx:
        def sb(name, shape, dt=fp32):
            return ctx.enter_context(nc.sbuf_tensor(name, shape, dt))

        def pb(name, shape):
            return ctx.enter_context(nc.psum_tensor(name, shape, fp32))

        def sem(name):
            return ctx.enter_context(nc.semaphore(name))

        wx = sb("wx", [P, HALVES, SLABS, 3, SLAB])
        cx = sb("cx", [P, HALVES, SLABS, 3, SLAB])
        urz = sb("urz", [P, HALVES, SLABS, 2, SLAB])
        uh = sb("uh", [P, HALVES, SLABS, SLAB])
        wz1 = sb("wz1", [P, HALVES, SLABS, SLAB])
        wh1 = sb("wh1", [P, HALVES, SLABS, SLAB])
        bias_rows = sb("bias_rows", [P, 4, SLAB])
        cond_f = sb("cond_f", [P, HALVES, B])
        leak = sb("leak", [P, HALVES, B])
        const_row = sb("const_row", [P, 4, SLAB])
        rest1 = sb("rest1", [P, 4, SLAB])
        rest2 = sb("rest2", [P, 4, SLAB])
        const_parts = [sb(f"const_part{n}", [P, 4, SLAB], bf16) for n in range(3)]
        const_stack = sb("const_stack", [3 * B, SLABS, 4 * SLAB], bf16)
        ident = sb("ident", [3 * B, B], bf16)

        x_in = sb("x_in", [P, 2, SLOT, HALVES, B])
        r_gate = sb("r_gate", [P, 2, SLAB])
        zero_z = sb("zero_z", [P, 2, SLAB, 2])
        cand_kept = sb("cand_kept", [P, 2, SLAB, 2])
        none_h = sb("none_h", [P, 2, SLAB, 2])
        h_f = sb("h_f", [P, 2, HALVES, B])
        x1_f = sb("x1_f", [P, 2, HALVES, B])
        rh = sb("rh", [P, 2, SLAB])
        rh_f = sb("rh_f", [P, 2, HALVES, B])
        zh = sb("zh", [P, 2, SLAB])
        gate = sb("gate", [P, 2, SLAB])
        gate_f = sb("gate_f", [P, 2, HALVES, B])
        gx = sb("gx", [P, 2, HALVES, B])
        leaked = sb("leaked", [P, 2, HALVES, B])
        pre1 = sb("pre1", [P, 2, HALVES, B])
        h1_f = sb("h1_f", [P, 2, HALVES, B])
        x2 = sb("x2", [P, HALVES, B, T])

        wl2 = sb("wl2", [P, HALVES, 3, HALVES, P])
        bl2 = sb("bl2", [P, 3, HALVES])
        wdown = sb("wdown", [P, HALVES, HALVES, P])
        wup = sb("wup", [P, HALVES, HALVES, P])
        w1 = sb("w1", [P, HALVES, HALVES, P])
        bias1 = sb("bias1", [P, HALVES])
        rank_rows = sb("rank_rows", [P, 4, 512])
        cond_rows = sb("cond_rows", [P, D])
        cond_slab = sb("cond_slab", [P, SLAB])
        gamma = sb("gamma", [P, SLAB])
        beta = sb("beta", [P, SLAB])
        stats = sb("stats", [P, 6])
        mean_var = sb("mean_var", [P, 2])
        var_eps = sb("var_eps", [P, 1])
        std = sb("std", [P, 1])
        rstd = sb("rstd", [P, 1])
        normed = sb("normed", [P, SLAB])
        scaled = sb("scaled", [P, SLAB])
        ada = sb("ada", [P, SLAB])
        ada_f = sb("ada_f", [P, HALVES, B])
        hid_f = sb("hid_f", [P, HALVES, B])
        rank_in = sb("rank_in", [P, 2, R, HALVES, B])

        arena = [sb(f"arena{n}", [P, 8 * COLS]) for n in range(4)]
        w2 = [space[:].rearrange("p (h j n) -> p h j n", h=HALVES, j=SLABS) for space in arena]
        pair = lambda space, at: space[:, 2 * at * COLS:2 * (at + 1) * COLS].rearrange("p (k c) -> p k c", k=2)
        f_t, i_t, c_t, rec = [pair(arena[0], n) for n in range(4)]
        ic, ni = [pair(arena[1], n) for n in range(2)]
        old = [w[:].rearrange("p a b c e -> p (a b c e)")[:, n * COLS:(n + 1) * COLS]
               for w, count in ((wx, 3), (cx, 3), (urz, 2)) for n in range(count)]
        old += [w[:].rearrange("p a b e -> p (a b e)") for w in (uh, wz1, wh1)]
        s_t, fn, fe, wrev, dec, wn, csum, hid2 = old[:8]
        rout_g = [old[8 + n].rearrange("p (w d) -> p w d", w=2) for n in range(2)]
        u_s, v_s = old[10][:, 0:T], old[10][:, T:2 * T]
        x3 = arena[2][:].rearrange("p (a h q t) -> p a h q t", a=2, h=HALVES, q=GB)
        rin_g = sb("rin_g", [P, 2, 2, HALVES, GB, BLK])
        mid = arena[1][:, 4 * COLS:8 * COLS].rearrange("p (q h t) -> p q h t", q=GB, h=HALVES)
        rank_out = arena[3][:].rearrange("p (w g d) -> p w g d", w=2, g=GROUPS)
        y = sb("y", [P, 2, HALVES, T])

        banks = [pb(f"bank{n}", [P, 512]) for n in range(8)]
        pre_a = banks[0:2]
        pre_g = banks[2:4]

        first_in, wx_in, weights_in = sem("first_in"), sem("wx_in"), sem("weights_in")
        adapter_in, tail_in = sem("adapter_in"), sem("tail_in")
        w2_in = [sem(f"w2_in{n}") for n in range(4)]
        ident_zero, ident_done, stack_done = sem("ident_zero"), sem("ident_done"), sem("stack_done")
        x_loaded = [sem("x_loaded0"), sem("x_loaded1")]
        const_pre, const_row_done, part_done, rest_done = (
            sem("const_pre"), sem("const_row_done"), sem("part_done"), sem("rest_done"))
        first_pre, first_z, first_cand = (
            sem("first_pre"), sem("first_z"), sem("first_cand"))
        zero_done = sem("zero_done")
        leak_done = sem("leak_done")
        rz_pre, cand_pre, gate_pre = sem("rz_pre"), sem("cand_pre"), sem("gate_pre")
        r_done, z_done, cand_done, gate_done, h1_done = sem("r_done"), sem("z_done"), sem("cand_done"), sem("gate_done"), sem("h1_done")
        rh_done, rhf_done, zh_done, kept_done = sem("rh_done"), sem("rhf_done"), sem("zh_done"), sem("kept_done")
        gatef_done, gx_done, pre1_done = sem("gatef_done"), sem("gx_done"), sem("pre1_done")
        h_done, hf_done, x1_done = sem("h_done"), sem("hf_done"), sem("x1_done")
        leaked_done, x2_done = sem("leaked_done"), sem("x2_done")

        ln_step, std_done, ada_done, hid_pre, hid_done = (
            sem("ln_step"), sem("std_done"), sem("ada_done"), sem("hid_pre"), sem("hid_done"))
        w2_used, rows_done, rin_done = (
            sem("w2_used"), sem("rows_done"), sem("rin_done"))
        scratch_out, rout_in = sem("scratch_out"), sem("rout_in")
        pad_done = sem("pad_done")

        l2_pre, f_done, i_done, c_done = sem("l2_pre"), sem("f_done"), sem("i_done"), sem("c_done")
        s_done, rec_done, fn_done, fe_done, ic_done, ni_done = (
            sem("s_done"), sem("rec_done"), sem("fn_done"), sem("fe_done"), sem("ic_done"), sem("ni_done"))
        wrev_done, wn_done, csum_done, dec_done, hid2_done, x3_done = (
            sem("wrev_done"), sem("wn_done"), sem("csum_done"), sem("dec_done"), sem("hid2_done"), sem("x3_done"))
        stage_done = sem("stage_done")
        u_pre, u_done, mid_pre, mid_done, v_pre, v_done, out_pre, y_done = (
            sem("u_pre"), sem("u_done"), sem("mid_pre"), sem("mid_done"), sem("v_pre"), sem("v_done"),
            sem("out_pre"), sem("y_done"))
        y_stored = [sem("y_stored0"), sem("y_stored1")]

        FIRST_LOADS = [(cond_f, "cond_f"), (cx, "cx"), (bias_rows, "bias_rows"), (leak, "alpha")]
        WEIGHT_LOADS = [(urz, "urz"), (uh, "uh"), (wz1, "wz1"), (wh1, "wh1")]
        ADAPTER_LOADS = [(cond_rows, "cond_rows"), (cond_slab, "cond_slab"), (gamma, "gamma"), (beta, "beta"),
                         (w1, "w1"), (bias1, "bias1")]
        TAIL_LOADS = [(rank_rows, "bias2_rows"), (wl2, "wl2"), (bl2, "bl2"), (wdown, "wdown"), (wup, "wup")]
        TURNS = T // BODY
        BREAK = TURNS // 2
        STAGED = 6
        scratch = io["scratch"]

        block = ctx.enter_context(nc.Block())

        @block.sync
        def _(sp):
            for dst, name in FIRST_LOADS:
                sp.dma_start(dst[:], io[name]).then_inc(first_in, 16)
            sp.dma_start(wx[:], io["wx"]).then_inc(wx_in, 16)
            for s in range(2):
                sp.dma_start(x_in[:, s], io["x"][:, s * SLOT:(s + 1) * SLOT]).then_inc(x_loaded[s], 16)
            for dst, name in WEIGHT_LOADS:
                sp.dma_start(dst[:], io[name]).then_inc(weights_in, 16)

            def next_steps(n, s):
                sp.wait_ge(x1_done, n * BODY + (s + 1) * SLOT)
                sp.dma_start(x_in[:, s], io["x"][:, bass.ds(n * BODY + BODY + s * SLOT, SLOT)]
                             ).then_inc(x_loaded[s], 16)

            for s in range(2):
                next_steps(0, s)
                for dst, name in TAIL_LOADS[s::2]:
                    sp.dma_start(dst[:], io[name]).then_inc(tail_in, 16)
            for w in range(4):
                for s in range(2):
                    next_steps(w + 1, s)
                    sp.dma_start(w2[w][:, s], io["w2"][:, w, s]).then_inc(w2_in[w], 16)
            with sp.Fori(5, TURNS) as n:
                for s in range(2):
                    next_steps(n, s)

            sp.wait_ge(rows_done, 4)
            for q in range(SLABS):
                for w in range(2):
                    sp.dma_start(scratch[w, :, 2 * q:2 * q + 2, :].rearrange("b r d -> b (r d)"),
                                 rank_rows[32 * q:32 * q + 32, 2 + w, :]).then_inc(scratch_out, 16)
            sp.wait_ge(scratch_out, 16 * 2 * SLABS)
            sp.wait_ge(pad_done, 2)
            for q in range(GB):
                for w in range(2):
                    sp.dma_start(rank_out[32 * q:32 * q + R, w],
                                 scratch[w].rearrange("(g q) r d -> q r g d", q=GB)[q]).then_inc(rout_in, 16)

            sp.sem_inc(y_stored[0], 1)
            sp.sem_inc(y_stored[1], 1)
            with sp.Fori(0, GROUPS) as g:
                for q in range(GB):
                    sp.wait_ge(y_done, g * GB + q + 2)
                    sp.dma_start(io["out"][:, :, bass.ds(g * GB + q, 1), :].rearrange("p h o t -> p h (o t)"),
                                 y[:, q % 2]).then_inc(y_stored[q % 2], 16)
            for s in range(2):
                sp.wait_ge(y_stored[s], 16 * B // 2 + 1)

        @block.gpsimd
        def _(pool):
            pool.memset(ident[:], 0.0).then_inc(ident_zero, 1)
            pool.wait_ge(ident_zero, 1)
            for part in range(3):
                eye = ident[part * B:(part + 1) * B, :]
                pool.affine_select(out=eye, in_=eye, compare_op=ALU.not_equal, fill=1.0, base=0,
                                   pattern=[[-1, B]], channel_multiplier=1).then_inc(ident_done, 1)
            pool.wait_ge(ident_done, 3)
            pool.memset(rin_g[:], 0.0).then_inc(pad_done, 1)
            pool.sem_inc(x2_done, 1)
            pool.sem_inc(y_done, 1)
            pool.wait_ge(leak_done, 1)
            pool.tensor_tensor(leaked[:, 0], leak[:], cond_f[:], ALU.mult).then_inc(leaked_done, 1)
            def turn(n):
                for u in range(BODY):
                    t = n * BODY + u
                    pool.wait_ge(h1_done, t + 2)
                    pool.tensor_tensor(leaked[:, (u + 1) % 2], leak[:], h1_f[:, u % 2],
                                       ALU.mult).then_inc(leaked_done, 1)
                    pool.tensor_tensor(x2[:, :, :, t], x1_f[:, u % 2], h1_f[:, u % 2],
                                       ALU.add).then_inc(x2_done, 1)

            with pool.Fori(0, BREAK) as n:
                turn(n)
            pool.wait_ge(w2_used, 4)
            pool.memset(rank_out, 0.0).then_inc(pad_done, 1)
            with pool.Fori(BREAK, TURNS) as n:
                turn(n)
            pool.wait_ge(pad_done, 2)

            def new_info(p, units):
                for unit in units:
                    k, c = unit % 2, p * 4 + unit
                    pool.wait_ge(c_done, c + 1)
                    pool.tensor_tensor(ic[:, k], i_t[:, k], c_t[:, k], ALU.mult).then_inc(ic_done, 1)
                    pool.wait_ge(rec_done, c + 1)
                    pool.wait_ge(ic_done, c + 1)
                    pool.tensor_tensor(ni[:, k], ic[:, k], rec[:, k], ALU.mult).then_inc(ni_done, 1)

            def factors(g, par):
                for w in range(2):
                    for half in range(HALVES):
                        pool.tensor_copy(rin_g[:, par, w, half, :, 0:R],
                                         rank_in[:, w, :, half, bass.ds(g * GB, GB)].rearrange("p r q -> p q r")
                                         ).then_inc(stage_done, 1)
                    pool.tensor_copy(rout_g[par][:, w, :], rank_out[:, w, bass.ds(g, 1), :]
                                     .rearrange("p o d -> p (o d)")).then_inc(stage_done, 1)

            def phase(p, par):
                new_info(p, range(2))
                pool.wait_ge(y_done, p * GB - GB + 1)
                factors(p, par)
                new_info(p, range(2, 4))

            new_info(0, range(4))
            pool.wait_ge(rin_done, 2)
            pool.wait_ge(rout_in, 16 * 2 * GB)
            factors(0, 0)
            new_info(1, range(2))
            factors(1, 1)
            new_info(1, range(2, 4))
            with pool.Fori(0, (GROUPS - 2) // 2) as n:
                phase(2 * n + 2, 0)
                phase(2 * n + 3, 1)

        @block.scalar
        def _(act):
            for dst, name in ADAPTER_LOADS:
                act.dma_start(dst[:], io[name]).then_inc(adapter_in, 16)
            act.wait_ge(ln_step, 3)
            act.activation(std[:], var_eps[:], ACT.Sqrt).then_inc(std_done, 1)
            act.wait_ge(hid_pre, 1)
            for m in range(HALVES):
                act.activation(hid_f[:, m], banks[4][:, m * B:(m + 1) * B], ACT.Gelu,
                               bias=bias1[:, m:m + 1]).then_inc(hid_done, 1)
            act.wait_ge(part_done, 1)
            for j in range(SLABS):
                act.activation(const_stack[0:B, j, :],
                               const_parts[0][j * B:(j + 1) * B].rearrange("p a e -> p (a e)"),
                               ACT.Copy).then_inc(stack_done, 1)
            act.wait_ge(first_pre, 1)
            act.wait_ge(zero_done, 1)
            act.activation(zero_z[:, 0, :, 1], pre_a[0][:, SLAB:2 * SLAB], ACT.Sigmoid).then_inc(first_z, 1)
            act.activation(cand_kept[:, 0, :, 0], pre_a[0][:, 2 * SLAB:3 * SLAB], ACT.Tanh).then_inc(first_cand, 1)
            with act.Fori(0, TURNS) as n:
                for u in range(BODY):
                    t, now, nxt = n * BODY + u, u % 2, (u + 1) % 2
                    act.wait_ge(rz_pre, t + 1)
                    for half in range(HALVES):
                        e = slice(half * BLK, (half + 1) * BLK)
                        act.activation(r_gate[:, nxt, e], pre_a[nxt][:, e], ACT.Sigmoid).then_inc(r_done, 1)
                    act.activation(zero_z[:, nxt, :, 1], pre_a[nxt][:, SLAB:2 * SLAB],
                                   ACT.Sigmoid).then_inc(z_done, 1)
                    act.wait_ge(gate_pre, t + 1)
                    act.activation(gate[:, now], pre_g[now][:, 0:SLAB], ACT.Sigmoid).then_inc(gate_done, 1)
                    act.wait_ge(cand_pre, t + 1)
                    for half in range(HALVES):
                        e = slice(half * BLK, (half + 1) * BLK)
                        act.activation(cand_kept[:, nxt, e, 0],
                                       pre_a[nxt][:, 2 * SLAB + half * BLK:2 * SLAB + (half + 1) * BLK],
                                       ACT.Tanh).then_inc(cand_done, 1)
                    act.wait_ge(pre1_done, t + 1)
                    act.activation(h1_f[:, now], pre1[:, now], ACT.Tanh).then_inc(h1_done, 1)

            def gates(p, units, first=False):
                for unit in units:
                    k, c, m = unit % 2, p * 4 + unit, unit % 2
                    for mat, (dst, fun, done) in enumerate(
                            ((f_t, ACT.Sigmoid, f_done), (i_t, ACT.Sigmoid, i_done), (c_t, ACT.Identity, c_done))):
                        act.wait_ge(l2_pre, p * 12 + unit * 3 + mat + 1)
                        if mat == 0 and not (first and unit < 2):
                            act.wait_ge(fn_done, c - 1)
                            act.wait_ge(ic_done, c - 1)
                        act.activation(dst[:, k], banks[(unit * 3 + mat) % 4][:], fun,
                                       bias=bl2[:, mat, m:m + 1]).then_inc(done, 1)

            def hidden_layer(g):
                act.wait_ge(u_pre, g + 1)
                act.activation(u_s, banks[4][:, 0:T], ACT.Copy).then_inc(u_done, 1)
                for q in range(GB):
                    act.wait_ge(mid_pre, g * GB + q + 1)
                    act.activation(mid[:, q].rearrange("p h t -> p (h t)"), banks[5 + q % 3][:],
                                   ACT.Gelu).then_inc(mid_done, 1)

            def ranks_out(g):
                act.wait_ge(v_pre, g + 1)
                act.activation(v_s, banks[4][:, 0:T], ACT.Copy).then_inc(v_done, 1)

            gates(0, range(4), first=True)
            with act.Fori(0, GROUPS - 1) as n:
                gates(n + 1, range(2))
                hidden_layer(n)
                gates(n + 1, range(2, 3))
                ranks_out(n)
                gates(n + 1, range(3, 4))
            hidden_layer(GROUPS - 1)
            ranks_out(GROUPS - 1)

        @block.vector
        def _(dve):
            dve.wait_ge(adapter_in, 16 * len(ADAPTER_LOADS))
            dve.bn_stats(stats[:], cond_rows[:]).then_inc(ln_step, 1)
            dve.wait_ge(ln_step, 1)
            dve.bn_aggr(mean_var[:], stats[:]).then_inc(ln_step, 1)
            dve.wait_ge(ln_step, 2)
            dve.tensor_scalar(var_eps[:], mean_var[:, 1:2], LN_EPS, None, ALU.add).then_inc(ln_step, 1)
            dve.wait_ge(std_done, 1)
            dve.reciprocal(rstd[:], std[:]).then_inc(ln_step, 1)
            dve.wait_ge(ln_step, 4)
            dve.tensor_scalar(normed[:], cond_slab[:], mean_var[:, 0:1], rstd[:, 0:1],
                              ALU.subtract, ALU.mult).then_inc(ln_step, 1)
            dve.wait_ge(ln_step, 5)
            dve.tensor_tensor(scaled[:], normed[:], gamma[:], ALU.mult).then_inc(ln_step, 1)
            dve.wait_ge(ln_step, 6)
            dve.tensor_tensor(ada[:], scaled[:], beta[:], ALU.add).then_inc(ln_step, 1)
            dve.wait_ge(ln_step, 7)
            dve.transpose(ada_f[:].rearrange("p h b -> p (h b)"), ada[:]).then_inc(ada_done, 1)
            dve.wait_ge(first_in, 16 * len(FIRST_LOADS))
            dve.memset(zero_z[:], 0.0).then_inc(zero_done, 1)
            dve.tensor_scalar(leak[:], leak[:], -1.0, 1.0, ALU.mult, ALU.add).then_inc(leak_done, 1)
            dve.tensor_copy(h1_f[:, 1], cond_f[:]).then_inc(h1_done, 1)
            dve.wait_ge(const_pre, 1)
            dve.tensor_tensor(const_row[:, 0:3].rearrange("p a e -> p (a e)"), pre_a[0][:, 0:192],
                              bias_rows[:, 0:3].rearrange("p a e -> p (a e)"), ALU.add).then_inc(const_row_done, 1)
            dve.tensor_copy(const_row[:, 3], bias_rows[:, 3]).then_inc(const_row_done, 1)
            dve.wait_ge(const_row_done, 2)
            dve.tensor_copy(const_parts[0][:], const_row[:]).then_inc(part_done, 1)
            dve.wait_ge(part_done, 1)
            dve.tensor_tensor(rest1[:], const_row[:], const_parts[0][:], ALU.subtract).then_inc(rest_done, 1)
            dve.wait_ge(rest_done, 1)
            dve.tensor_copy(const_parts[1][:], rest1[:]).then_inc(part_done, 1)
            dve.wait_ge(part_done, 2)
            dve.tensor_tensor(rest2[:], rest1[:], const_parts[1][:], ALU.subtract).then_inc(rest_done, 1)
            dve.wait_ge(rest_done, 2)
            dve.tensor_copy(const_parts[2][:], rest2[:]).then_inc(part_done, 1)
            dve.wait_ge(part_done, 3)
            for part in (1, 2):
                for j in range(SLABS):
                    dve.tensor_copy(const_stack[part * B:(part + 1) * B, j, :],
                                    const_parts[part][j * B:(j + 1) * B].rearrange("p a e -> p (a e)")
                                    ).then_inc(stack_done, 1)
            dve.wait_ge(first_cand, 1)
            dve.tensor_tensor(none_h[:, 0, :, 1], zero_z[:, 0, :, 1], cand_kept[:, 0, :, 0],
                              ALU.mult).then_inc(h_done, 1)
            dve.wait_ge(h_done, 1)
            dve.transpose(h_f[:, 0].rearrange("p h b -> p (h b)"), none_h[:, 0, :, 1]).then_inc(hf_done, 2)
            dve.wait_ge(x_loaded[0], 16)
            dve.wait_ge(hf_done, 2)
            dve.tensor_tensor(x1_f[:, 0], x_in[:, 0, 0], h_f[:, 0], ALU.add).then_inc(x1_done, 1)

            def turn(n):
                for u in range(BODY):
                    t, now, nxt = n * BODY + u, u % 2, (u + 1) % 2
                    slot, at = ((u + 1) // SLOT) % 2, (u + 1) % SLOT
                    for half in range(HALVES):
                        e = slice(half * BLK, (half + 1) * BLK)
                        dve.wait_ge(r_done, 2 * t + half + 1)
                        dve.tensor_tensor(rh[:, nxt, e], r_gate[:, nxt, e], none_h[:, now, e, 1],
                                          ALU.mult).then_inc(rh_done, 1)
                    for half in range(HALVES):
                        dve.wait_ge(rh_done, 2 * t + half + 1)
                        dve.transpose(rh_f[:, nxt, half], rh[:, nxt, half * BLK:(half + 1) * BLK]
                                      ).then_inc(rhf_done, 1)
                    dve.wait_ge(z_done, t + 1)
                    dve.tensor_tensor(zh[:, nxt], zero_z[:, nxt, :, 1], none_h[:, now, :, 1],
                                      ALU.mult).then_inc(zh_done, 1)
                    dve.wait_ge(zh_done, t + 1)
                    dve.tensor_tensor(cand_kept[:, nxt, :, 1], none_h[:, now, :, 1], zh[:, nxt],
                                      ALU.subtract).then_inc(kept_done, 1)
                    dve.wait_ge(gate_done, t + 1)
                    dve.transpose(gate_f[:, now].rearrange("p h b -> p (h b)"), gate[:, now]).then_inc(gatef_done, 1)
                    dve.wait_ge(gatef_done, t + 1)
                    dve.tensor_tensor(gx[:, now], gate_f[:, now], x1_f[:, now], ALU.mult).then_inc(gx_done, 1)
                    for half in range(HALVES):
                        e = slice(half * BLK, (half + 1) * BLK)
                        dve.wait_ge(cand_done, 2 * t + half + 1)
                        if half == 0:
                            dve.wait_ge(kept_done, t + 1)
                        dve.tensor_tensor_scan(none_h[:, nxt, e].rearrange("p e a -> p (e a)"),
                                               zero_z[:, nxt, e].rearrange("p e a -> p (e a)"),
                                               cand_kept[:, nxt, e].rearrange("p e a -> p (e a)"),
                                               0.0, ALU.mult, ALU.add).then_inc(h_done, 1)
                    for half in range(HALVES):
                        dve.wait_ge(h_done, 2 * t + half + 2)
                        dve.transpose(h_f[:, nxt, half], none_h[:, nxt, half * BLK:(half + 1) * BLK, 1]
                                      ).then_inc(hf_done, 1)
                    dve.wait_ge(gx_done, t + 1)
                    dve.wait_ge(leaked_done, t + 1)
                    dve.tensor_tensor(pre1[:, now], gx[:, now], leaked[:, now], ALU.add).then_inc(pre1_done, 1)
                    if at == 0:
                        dve.wait_ge(x_loaded[slot], (n + 1 + (1 if slot == 0 else 0)) * 16)
                    dve.wait_ge(x2_done, t + 1)
                    dve.wait_ge(hf_done, 2 * t + 4)
                    dve.tensor_tensor(x1_f[:, nxt], x_in[:, slot, at], h_f[:, nxt], ALU.add).then_inc(x1_done, 1)

            with dve.Fori(0, BREAK) as n:
                turn(n)
            dve.wait_ge(tail_in, 16 * len(TAIL_LOADS))
            for w in range(4):
                dve.wait_ge(w2_used, w + 1)
                dve.tensor_tensor(rank_rows[:, w], banks[4 + w][:], rank_rows[:, w], ALU.add).then_inc(rows_done, 1)
            for w in range(2):
                dve.wait_ge(rows_done, w + 1)
                dve.transpose(rank_in[:, w].rearrange("p r h b -> p (r h b)"), rank_rows[:, w]).then_inc(rin_done, 1)
            with dve.Fori(BREAK, TURNS) as n:
                turn(n)

            def scan_unit(p, unit, par):
                k, c, m, hf = unit % 2, p * 4 + unit, unit % 2, unit // 2
                dve.wait_ge(i_done, c + 1)
                dve.scalar_tensor_tensor(s_t, f_t[:, k], EPS, i_t[:, k], ALU.add, ALU.add).then_inc(s_done, 1)
                dve.wait_ge(s_done, c + 1)
                dve.reciprocal(rec[:, k], s_t).then_inc(rec_done, 1)
                dve.wait_ge(rec_done, c + 1)
                dve.tensor_tensor(fn, f_t[:, k], rec[:, k], ALU.mult).then_inc(fn_done, 1)
                dve.wait_ge(fn_done, c + 1)
                dve.tensor_scalar(fe, fn, EPS, None, ALU.add).then_inc(fe_done, 1)
                dve.wait_ge(fe_done, c + 1)
                for b in range(2):
                    rev = slice(b * T, (b + 1) * T)
                    dve.tensor_tensor_scan(wrev[:, rev][:, ::-1], fe[:, rev][:, ::-1], fe[:, rev][:, ::-1],
                                           1.0, ALU.mult, ALU.bypass).then_inc(wrev_done, 1)
                for b in range(2):
                    col = slice(b * T, (b + 1) * T)
                    dve.tensor_tensor_scan(dec[:, col], fe[:, col], fe[:, col],
                                           cond_f[:, m, bass.ds(p * GB + 2 * hf + b, 1)],
                                           ALU.mult, ALU.bypass).then_inc(dec_done, 1)
                dve.wait_ge(wrev_done, 2 * c + 2)
                dve.wait_ge(ni_done, c + 1)
                dve.tensor_tensor(wn, wrev, ni[:, k], ALU.mult).then_inc(wn_done, 1)
                dve.wait_ge(wn_done, c + 1)
                for b in range(2):
                    col = slice(b * T, (b + 1) * T)
                    dve.tensor_tensor_scan(csum[:, col], wn[:, col], wn[:, col],
                                           0.0, ALU.add, ALU.bypass).then_inc(csum_done, 1)
                dve.wait_ge(csum_done, 2 * c + 2)
                dve.wait_ge(dec_done, 2 * c + 2)
                dve.tensor_tensor(hid2, csum, dec, ALU.add).then_inc(hid2_done, 1)
                dve.wait_ge(hid2_done, c + 1)
                dve.tensor_tensor(x3[:, par, m, 2 * hf:2 * hf + 2, :].rearrange("p q t -> p (q t)"),
                                  x2[:, m, bass.ds(p * GB + 2 * hf, 2), :].rearrange("p q t -> p (q t)"),
                                  hid2, ALU.add).then_inc(x3_done, 1)

            def outputs(g, qs, par):
                for q in qs:
                    dve.wait_ge(out_pre, g * GB + q + 1)
                    dve.wait_ge(y_stored[q % 2], (g * 2 + q // 2) * 16 + 1)
                    dve.scalar_tensor_tensor(y[:, q % 2], x3[:, par, :, q, :], 2.0,
                                             banks[5 + (GB + q) % 3][:].rearrange("p (h t) -> p h t", h=HALVES),
                                             ALU.mult, ALU.add).then_inc(y_done, 1)

            def phase(p, par):
                for unit in range(3):
                    scan_unit(p, unit, par)
                outputs(p - 1, range(2), 1 - par)
                scan_unit(p, 3, par)
                outputs(p - 1, range(2, 4), 1 - par)

            for unit in range(4):
                scan_unit(0, unit, 0)
            with dve.Fori(0, (GROUPS - 2) // 2) as n:
                phase(2 * n + 1, 1)
                phase(2 * n + 2, 0)
            phase(GROUPS - 1, 1)
            outputs(GROUPS - 1, range(GB), 1)

        @block.tensor
        def _(pe):
            def tiles(out, lo, n, stationary, moving, start=False, ready=None):
                for k in range(HALVES):
                    if ready:
                        ready(k)
                    for j in range(SLABS):
                        mm = pe.matmul(out[32 * j:32 * j + 32, lo:lo + n], stationary[:, k, :], moving(k, j),
                                       start=start and k == 0, stop=k == 1, tile_position=(0, 32 * j),
                                       skip_group_check=True)
                return mm

            def constants(out, lo, n):
                for j in range(SLABS):
                    mm = pe.matmul(out[32 * j:32 * j + 32, 0:n], ident[:], const_stack[:, j, lo:lo + n],
                                   start=True, stop=False, tile_position=(0, 32 * j), skip_group_check=True)
                return mm

            flat3 = lambda w: (lambda k, j: w[:, k, j].rearrange("p a e -> p (a e)"))
            flat1 = lambda w: (lambda k, j: w[:, k, j])

            pe.wait_ge(adapter_in, 16 * len(ADAPTER_LOADS))
            pe.wait_ge(ada_done, 1)
            for m in range(HALVES):
                for k in range(HALVES):
                    mm = pe.matmul(banks[4][:, m * B:(m + 1) * B], w1[:, k, m], ada_f[:, k],
                                   start=k == 0, stop=k == 1)
            mm.then_inc(hid_pre, 1)

            pe.wait_ge(first_in, 16 * len(FIRST_LOADS))
            tiles(pre_a[0], 0, 3 * SLAB, cond_f, flat3(cx), start=True).then_inc(const_pre, 1)
            pe.wait_ge(ident_done, 3)
            pe.wait_ge(stack_done, 3 * SLABS)
            pe.wait_ge(x_loaded[0], 16)
            pe.wait_ge(wx_in, 16)
            constants(pre_a[0], 0, 3 * SLAB)
            tiles(pre_a[0], 0, 3 * SLAB, x_in[:, 0, 0], flat3(wx)).then_inc(first_pre, 1)
            pe.wait_ge(weights_in, 16 * len(WEIGHT_LOADS))

            def turn(n):
                for u in range(BODY):
                    t, now, nxt = n * BODY + u, u % 2, (u + 1) % 2
                    slot, at = ((u + 1) // SLOT) % 2, (u + 1) % SLOT

                    def rh_ready(k):
                        pe.wait_ge(rhf_done, 2 * t + k + 1)
                        if k == 0:
                            pe.wait_ge(z_done, t + 1)

                    if at == 0:
                        pe.wait_ge(x_loaded[slot], (n + 1 + (1 if slot == 0 else 0)) * 16)
                    constants(pre_a[nxt], 0, 3 * SLAB)
                    tiles(pre_a[nxt], 0, 3 * SLAB, x_in[:, slot, at], flat3(wx))
                    tiles(pre_a[nxt], 0, 2 * SLAB, h_f[:, now], flat3(urz),
                          ready=lambda k: pe.wait_ge(hf_done, 2 * t + k + 1)).then_inc(rz_pre, 1)
                    constants(pre_g[now], 3 * SLAB, SLAB)
                    pe.wait_ge(x1_done, t + 1)
                    tiles(pre_g[now], 0, SLAB, x1_f[:, now], flat1(wz1))
                    pe.wait_ge(h1_done, t + 1)
                    tiles(pre_g[now], 0, SLAB, h1_f[:, nxt], flat1(wh1)).then_inc(gate_pre, 1)
                    tiles(pre_a[nxt], 2 * SLAB, SLAB, rh_f[:, nxt], flat1(uh),
                          ready=rh_ready).then_inc(cand_pre, 1)

            with pe.Fori(0, BREAK) as n:
                turn(n)
            pe.wait_ge(hid_done, 2)
            for w in range(4):
                pe.wait_ge(w2_in[w], 32)
                for k in range(HALVES):
                    for j in range(SLABS):
                        mm = pe.matmul(banks[4 + w][32 * j:32 * j + 32, :], hid_f[:, k], w2[w][:, k, j],
                                       start=k == 0, stop=k == 1, tile_position=(0, 32 * j))
                mm.then_inc(w2_used, 1)
            with pe.Fori(BREAK, TURNS) as n:
                turn(n)

            def gate_products(p, unit, first=False):
                m, hf = unit % 2, unit // 2
                for mat in range(3):
                    at = unit * 3 + mat
                    if at >= 4 or not first:
                        prev = at - 4 if at >= 4 else at + 8
                        unit_before = (p if at >= 4 else p - 1) * 4 + prev // 3
                        pe.wait_ge((f_done, i_done, c_done)[prev % 3], unit_before + 1)
                    for k in range(HALVES):
                        mm = pe.matmul(banks[at % 4][:], wl2[:, k, mat, m],
                                       x2[:, k, bass.ds(p * GB + 2 * hf, 2), :].rearrange("p q t -> p (q t)"),
                                       start=k == 0, stop=k == 1)
                    mm.then_inc(l2_pre, 1)

            def rank_products(par, w, moving, done):
                for k in range(HALVES):
                    for q in range(GB):
                        mm = pe.matmul(banks[4][32 * q:32 * q + 32, 0:T], rin_g[:, par, w, k, q], moving(k, q),
                                       start=k == 0, stop=k == 1, tile_position=(0, 32 * q))
                mm.then_inc(done, 1)

            def dense(par, q, bank, weights, moving, w, low):
                for m in range(HALVES):
                    for k in range(HALVES):
                        pe.matmul(banks[bank][:, m * T:(m + 1) * T], weights[:, k, m], moving(k, q),
                                  start=k == 0, stop=False, skip_group_check=True)
                    mm = pe.matmul(banks[bank][:, m * T:(m + 1) * T],
                                   rout_g[par][32 * q:32 * q + R, w, m * P:(m + 1) * P],
                                   low[32 * q:32 * q + R, :], start=False, stop=True,
                                   tile_position=(32 * q, 0), skip_group_check=True)
                return mm

            def down(g, par):
                pe.wait_ge(x3_done, g * 4 + 4)
                pe.wait_ge(stage_done, g * STAGED + STAGED)
                rank_products(par, 0, lambda k, q: x3[:, par, k, q], u_pre)
                pe.wait_ge(y_done, g * GB + 1)
                pe.wait_ge(u_done, g + 1)
                for q in range(GB):
                    if q == 3:
                        pe.wait_ge(mid_done, g * GB + 1)
                    dense(par, q, 5 + q % 3, wdown, lambda k, q: x3[:, par, k, q], 1, u_s).then_inc(mid_pre, 1)

            def up_ranks(g, par):
                pe.wait_ge(mid_done, g * GB + GB)
                rank_products(par, 1, lambda k, q: mid[:, q, k], v_pre)

            def up(g, par, qs):
                pe.wait_ge(v_done, g + 1)
                for q in qs:
                    if q == 3:
                        pe.wait_ge(y_done, g * GB + 2)
                    dense(par, q, 5 + (GB + q) % 3, wup, lambda k, q: mid[:, q, k], 0, v_s).then_inc(out_pre, 1)

            def phase(p, par):
                gate_products(p, 0)
                gate_products(p, 1)
                down(p - 1, 1 - par)
                gate_products(p, 2)
                up_ranks(p - 1, 1 - par)
                up(p - 1, 1 - par, range(2))
                gate_products(p, 3)
                up(p - 1, 1 - par, range(2, GB))

            pe.wait_ge(x2_done, T + 1)
            pe.wait_ge(cand_done, 2 * T)
            pe.wait_ge(gate_done, T)
            pe.wait_ge(tail_in, 16 * len(TAIL_LOADS))
            for unit in range(4):
                gate_products(0, unit, first=True)
            with pe.Fori(0, (GROUPS - 2) // 2) as n:
                phase(2 * n + 1, 1)
                phase(2 * n + 2, 0)
            phase(GROUPS - 1, 1)
            down(GROUPS - 1, 1)
            up_ranks(GROUPS - 1, 1)
            up(GROUPS - 1, 1, range(GB))


def _rows(w):
    n = w.shape[1]
    return w.reshape(SLABS, HALVES, BLK, n).transpose(0, 2, 1, 3).reshape(P, HALVES, n)


def _cols(w):
    s = w.shape[:-1]
    w = w.reshape(*s, SLABS, HALVES, BLK)
    n = len(s)
    return w.transpose(*range(n), n + 1, n, n + 2).reshape(*s, HALVES, P)


def _slabs(np, ws):
    return np.stack([_rows(w).reshape(P, HALVES, SLABS, SLAB) for w in ws], axis=3)


def _part(v):
    return v.reshape(SLABS, HALVES, BLK).transpose(0, 2, 1).reshape(P, HALVES)


def _by_slab(v):
    s = v.shape[:-2]
    n = len(s)
    v = v.reshape(*s, SLABS, HALVES, BLK, R)
    return v.transpose(*range(n), n, n + 3, n + 1, n + 2).reshape(*s, SLABS, 512)


def _by_rank(v):
    s = v.shape[:-2]
    v = _cols(v.swapaxes(-1, -2))
    return v.reshape(*s, SLABS, 512)


def kernel(**inputs):
    import numpy as np
    import concourse.bacc as bacc
    from concourse.bass_utils import run_bass_kernel_spmd

    a = {k: np.asarray(v) for k, v in inputs.items()}
    cond = a["cond_1024"]
    slab_rows = lambda v: np.repeat(v.reshape(SLABS, 1, SLAB), B, axis=1).reshape(P, SLAB)
    x = a["x"].reshape(B, T, SLABS, HALVES, BLK).transpose(2, 4, 1, 3, 0).reshape(P, T, HALVES, B)
    x_pad = np.zeros((P, T_PAD, HALVES, B), x.dtype)
    x_pad[:, :T] = x
    w2 = _rows(a["L3_cond_W2"]).reshape(P, HALVES, 4, D, R)
    factors = lambda v: np.stack([_by_slab(v[..., 2, :, :]), _by_slab(v[..., 1, :, :]),
                                  _by_rank(v[..., 0, :, :]), _by_rank(v[..., 3, :, :])], axis=-3)
    w2 = factors(w2).transpose(0, 2, 1, 3, 4)
    bias2 = factors(a["L3_cond_bias2"].reshape(4, D, R))
    host = {
        "x": x_pad,
        "wx": _slabs(np, [a["L0_cond_W_r"], a["L0_cond_W_z"], a["L0_cond_W"]]),
        "cx": _slabs(np, [a["L0_cond_C_r"], a["L0_cond_C_z"], a["L0_cond_C"]]),
        "urz": _slabs(np, [a["L0_cond_U_r"], a["L0_cond_U_z"]]),
        "uh": _slabs(np, [a["L0_cond_U"]])[:, :, :, 0],
        "wz1": _slabs(np, [a["L1_cond_W"][:, D:].T])[:, :, :, 0],
        "wh1": _slabs(np, [a["L1_cond_W"][:, :D].T])[:, :, :, 0],
        "bias_rows": np.stack([slab_rows(a[k]) for k in ("L0_cond_b_r", "L0_cond_b_z", "L0_cond_b", "L1_cond_b")],
                              axis=1),
        "cond_f": _rows(cond.T),
        "alpha": np.repeat(_part(a["L1_cond_alpha"])[:, :, None], B, axis=2),
        "wl2": np.stack([_cols(_rows(a[k].T)) for k in ("L2_cond_W_f", "L2_cond_W_i", "L2_cond_W_h")], axis=2),
        "bl2": np.stack([_part(a[k]) for k in ("L2_cond_b_f", "L2_cond_b_i", "L2_cond_b_h")], axis=1),
        "wdown": _cols(_rows(a["L3_cond_base_down"])),
        "wup": _cols(_rows(a["L3_cond_base_up"].T)),
        "w1": _cols(_rows(a["L3_cond_W1"])),
        "bias1": _part(a["L3_cond_bias1"]),
        "w2": w2,
        "bias2_rows": np.repeat(bias2.transpose(1, 0, 2)[:, None], B, axis=1).reshape(P, 4, 512),
        "cond_rows": np.concatenate([cond] * SLABS, axis=0),
        "cond_slab": cond.reshape(B, SLABS, SLAB).transpose(1, 0, 2).reshape(P, SLAB),
        "gamma": slab_rows(a["L3_cond_ln_gamma"]),
        "beta": slab_rows(a["L3_cond_ln_beta"]),
    }
    nc = bacc.Bacc("TRN2", target_bir_lowering=False, num_devices=1)
    arrays, io = {}, {}
    for name, v in host.items():
        v = np.ascontiguousarray(v)
        arrays[f"in_{name}"] = v
        io[name] = nc.dram_tensor(f"in_{name}", v.shape, mybir.dt.from_np(v.dtype), kind="ExternalInput").ap()
    io["scratch"] = nc.dram_tensor("scratch", (2, B, R, D), mybir.dt.float32, kind="Internal").ap()
    io["out"] = nc.dram_tensor("out_0", (P, HALVES, B, T), mybir.dt.float32, kind="ExternalOutput").ap()
    build_program(nc, io)
    r = run_bass_kernel_spmd(nc, [arrays], core_ids=[0])
    y = r.results[0]["out_0"]
    return y.reshape(SLABS, BLK, HALVES, B, T).transpose(3, 4, 0, 2, 1).reshape(B, T, D)
```
